# Optimizing a Trainium2 kernel written in Bass

```python
import numpy as np
import jax
import jax.numpy as jnp

def _softmax(x, axis=-1):
    return jax.nn.softmax(x, axis=axis)

def _gelu(x):
    return jax.nn.gelu(x, approximate=True)

def _silu(x):
    return jax.nn.silu(x)

def _sigmoid(x):
    return jax.nn.sigmoid(x)

def _layernorm(x, axis=-1, eps=1e-05):
    m = jnp.mean(x, axis=axis, keepdims=True)
    v = jnp.var(x, axis=axis, keepdims=True)
    return (x - m) / jnp.sqrt(v + eps)

def _scatter_add(tgt, idx, src, axis=0):
    return tgt.at[idx].add(src)

def _segment_sum(src, seg, n):
    return jax.ops.segment_sum(src, seg, n)
kernel_name = 'mk_gps_d1_gnn_r8_43831c'

def setup_inputs(seed: int=0):
    np.random.seed(seed)
    _w = jnp.asarray

    def _rec_inputs():
        import jax
        import jax.numpy as jnp
        _gk = jax.random.key(seed)
        x = -0.0002117 + 1 * jax.random.normal(jax.random.fold_in(_gk, 1), (6250, 256), jnp.float32)
        src = jax.random.randint(jax.random.fold_in(_gk, 2), (100000,), 0, 6250, jnp.int32)
        dst = jnp.minimum((6250 * jax.random.uniform(jax.random.fold_in(_gk, 3), (100000,)) ** 2.0).astype(jnp.int32), 49999)
        _o = jnp.argsort(dst, stable=True)
        src = src[_o]
        dst = dst[_o]
        return (x, src, dst)
    x, src, dst = _rec_inputs()

    def _L0_gnn_setup():
        import jax, jax.numpy as jnp
        import numpy as np
        N_NODES = 12500
        N_EDGES = 400000
        D_IN = 256
        D_OUT = 256
        key = jax.random.key(seed)
        k1, k2, k3, k4 = jax.random.split(key, 4)
        x = jax.random.normal(k1, (N_NODES, D_IN), dtype=jnp.float32)
        W = jax.random.normal(k2, (D_OUT, D_IN), dtype=jnp.float32) / np.sqrt(D_IN).astype(np.float32)
        bias = jnp.zeros((D_OUT,), dtype=jnp.float32)
        rows = jax.random.randint(k3, (N_EDGES,), 0, N_NODES, dtype=jnp.int32)
        cols = jax.random.randint(k4, (N_EDGES,), 0, N_NODES, dtype=jnp.int32)
        return {'x': x, 'W': W, 'bias': bias, 'rows': rows, 'cols': cols}
    _L0_gnn_all = _L0_gnn_setup()
    _L0_gnn_in = {k: v for k, v in _L0_gnn_all.items() if k in ('W', 'bias')}
    del _L0_gnn_all

    def _L0_mix_setup():
        import jax, jax.numpy as jnp
        import numpy as np
        B, N, C, H = (8, 2048, 256, 8)
        D = C // H
        GH = C // 4
        key = jax.random.key(seed)
        ks = jax.random.split(key, 6)
        s = 0.02
        return {'x': jax.random.normal(ks[0], (B, N, C), dtype=jnp.float32), 'Wqkv': jax.random.normal(ks[1], (C, 3 * C), dtype=jnp.float32) * s, 'Wproj': jax.random.normal(ks[2], (C, C), dtype=jnp.float32) * s, 'bproj': jnp.zeros((C,), dtype=jnp.float32), 'ln_g': jnp.ones((C,), dtype=jnp.float32), 'ln_b': jnp.zeros((C,), dtype=jnp.float32), 'Wg1': jax.random.normal(ks[3], (C, GH), dtype=jnp.float32) * s, 'bg1': jnp.zeros((GH,), dtype=jnp.float32), 'Wg2': jax.random.normal(ks[4], (GH, C), dtype=jnp.float32) * s, 'bg2': jnp.zeros((C,), dtype=jnp.float32)}
    _L0_mix_all = _L0_mix_setup()
    _L0_mix_in = {k: v for k, v in _L0_mix_all.items() if k in ('Wqkv', 'Wproj', 'bproj', 'ln_g', 'ln_b', 'Wg1', 'bg1', 'Wg2', 'bg2')}
    del _L0_mix_all

    def _L0_ffn_setup():
        import jax, jax.numpy as jnp
        import numpy as np
        B, S, D = (8, 512, 256)
        H = 4 * D
        CAPACITY = 0.5
        key = jax.random.key(seed)
        ks = jax.random.split(key, 6)
        x = jax.random.normal(ks[0], (B, S, D), dtype=jnp.float32)
        attention_mask = jnp.zeros((B, 1, 1, S), dtype=jnp.float32)
        wr = jax.random.normal(ks[1], (D, 1), dtype=jnp.float32) * 0.02
        br = jnp.zeros((1,), dtype=jnp.float32)
        w1 = jax.random.normal(ks[2], (D, H), dtype=jnp.float32) * 0.02
        b1 = jnp.zeros((H,), dtype=jnp.float32)
        w2 = jax.random.normal(ks[3], (H, D), dtype=jnp.float32) * 0.02
        b2 = jnp.zeros((D,), dtype=jnp.float32)
        return {'x': x, 'attention_mask': attention_mask, 'wr': wr, 'br': br, 'w1': w1, 'b1': b1, 'w2': w2, 'b2': b2}
    _L0_ffn_all = _L0_ffn_setup()
    _L0_ffn_in = {k: v for k, v in _L0_ffn_all.items() if k in ('attention_mask', 'wr', 'br', 'w1', 'b1', 'w2', 'b2')}
    del _L0_ffn_all
    return {'x': x, 'src': src, 'dst': dst, 'L0_gnn_W': _L0_gnn_in['W'], 'L0_gnn_bias': _L0_gnn_in['bias'], 'L0_mix_Wqkv': _L0_mix_in['Wqkv'], 'L0_mix_Wproj': _L0_mix_in['Wproj'], 'L0_mix_bproj': _L0_mix_in['bproj'], 'L0_mix_ln_g': _L0_mix_in['ln_g'], 'L0_mix_ln_b': _L0_mix_in['ln_b'], 'L0_mix_Wg1': _L0_mix_in['Wg1'], 'L0_mix_bg1': _L0_mix_in['bg1'], 'L0_mix_Wg2': _L0_mix_in['Wg2'], 'L0_mix_bg2': _L0_mix_in['bg2'], 'L0_ffn_attention_mask': _L0_ffn_in['attention_mask'], 'L0_ffn_wr': _L0_ffn_in['wr'], 'L0_ffn_br': _L0_ffn_in['br'], 'L0_ffn_w1': _L0_ffn_in['w1'], 'L0_ffn_b1': _L0_ffn_in['b1'], 'L0_ffn_w2': _L0_ffn_in['w2'], 'L0_ffn_b2': _L0_ffn_in['b2']}

def reference(x, src, dst, L0_gnn_W, L0_gnn_bias, L0_mix_Wqkv, L0_mix_Wproj, L0_mix_bproj, L0_mix_ln_g, L0_mix_ln_b, L0_mix_Wg1, L0_mix_bg1, L0_mix_Wg2, L0_mix_bg2, L0_ffn_attention_mask, L0_ffn_wr, L0_ffn_br, L0_ffn_w1, L0_ffn_b1, L0_ffn_w2, L0_ffn_b2):
    import jax
    import jax.numpy as jnp

    def _L0_gnn_ref(x, W, bias, rows, cols):
        import jax, jax.numpy as jnp
        import numpy as np
        N_NODES = 12500
        N_EDGES = 400000
        D_IN = 256
        D_OUT = 256
        n = x.shape[0]
        h = x @ W.T + bias
        deg = jax.ops.segment_sum(jnp.ones(rows.shape, x.dtype), rows, num_segments=n)
        norm = jax.lax.rsqrt(1.0 + deg)[:, None]
        h = norm * h
        agg = jax.ops.segment_sum(h[cols], rows, num_segments=n)
        h = agg + h
        return norm * h

    def _L0_mix_ref(x, Wqkv, Wproj, bproj, ln_g, ln_b, Wg1, bg1, Wg2, bg2):
        import jax, jax.numpy as jnp
        import numpy as np
        B, N, C, H = (8, 2048, 256, 8)
        D = C // H
        GH = C // 4
        b, n, c = x.shape
        h, d = (H, D)
        qkv = (x @ Wqkv).reshape(b, n, 3, h, d)
        q, k, v = (qkv[:, :, 0], qkv[:, :, 1], qkv[:, :, 2])
        k = jax.nn.softmax(k, axis=1)
        context = jnp.einsum('bnhd,bnhv->bhdv', k, v)
        out = jnp.einsum('bnhd,bhdv->bnhv', q, context).reshape(b, n, c)
        mu = jnp.mean(x, axis=-1, keepdims=True)
        var = jnp.var(x, axis=-1, keepdims=True)
        xn = (x - mu) * jax.lax.rsqrt(var + 1e-05) * ln_g + ln_b
        hgate = jax.nn.gelu(xn @ Wg1 + bg1, approximate=False)
        gate = jax.nn.sigmoid(hgate @ Wg2 + bg2)
        return out * gate @ Wproj + bproj

    def _L0_ffn_ref(x, attention_mask, wr, br, w1, b1, w2, b2):
        import jax, jax.numpy as jnp
        import numpy as np
        B, S, D = (8, 512, 256)
        H = 4 * D
        CAPACITY = 0.5
        b, s, d = x.shape
        weights = (jnp.einsum('bsd,do->bso', x, wr) + br)[..., 0]
        k = max(1, int(CAPACITY * s))
        kk = k - 1 if k > 1 else 1
        _, idx = jax.lax.top_k(weights, k)
        sel_idx = idx[:, :kk]
        sel = jnp.take_along_axis(x, sel_idx[:, :, None], axis=1)
        h = jax.nn.gelu(jnp.einsum('bkd,dh->bkh', sel, w1) + b1)
        y = jnp.einsum('bkh,hd->bkd', h, w2) + b2
        w_sel = jnp.take_along_axis(weights, sel_idx, axis=1)
        y = y * w_sel[..., None]
        batch_idx = jnp.arange(b)[:, None]
        processed = jnp.zeros_like(x).at[batch_idx, sel_idx].set(y)
        return processed + x
    xn = _layernorm(x, axis=-1)
    x = x + _L0_gnn_ref(xn, L0_gnn_W, L0_gnn_bias, src, dst) + _L0_mix_ref(xn[None], L0_mix_Wqkv, L0_mix_Wproj, L0_mix_bproj, L0_mix_ln_g, L0_mix_ln_b, L0_mix_Wg1, L0_mix_bg1, L0_mix_Wg2, L0_mix_bg2)[0]
    x = x + _L0_ffn_ref(_layernorm(x, axis=-1)[None], L0_ffn_attention_mask, L0_ffn_wr, L0_ffn_br, L0_ffn_w1, L0_ffn_b1, L0_ffn_w2, L0_ffn_b2)[0]
    return x

_drawn_inputs = setup_inputs


def setup_inputs(seed=0):
    import zlib

    import numpy as np

    out = dict(_drawn_inputs(seed))
    spreads = {'L0_gnn_bias': (0.0, 0.8),
     'L0_mix_bproj': (0.0, 0.8),
     'L0_mix_ln_g': (1.0, 0.6),
     'L0_mix_ln_b': (0.0, 0.8),
     'L0_mix_bg1': (0.0, 0.8),
     'L0_mix_bg2': (0.0, 0.8),
     'L0_ffn_b1': (0.0, 0.8),
     'L0_ffn_b2': (0.0, 0.8)}
    factors = {'L0_mix_Wqkv': 8.0,
     'L0_mix_Wproj': 8.0,
     'L0_mix_Wg1': 8.0,
     'L0_mix_Wg2': 8.0,
     'L0_ffn_wr': 3.987,
     'L0_ffn_w1': 5.309,
     'L0_ffn_w2': 4.958,
     'L0_gnn_W': 2.818}
    for name, (base, spread) in spreads.items():
        noise = np.random.default_rng([zlib.crc32(name.encode()), seed]).standard_normal(out[name].shape)
        drawn = base * np.exp(spread * noise) if base else spread * noise
        out[name] = jnp.asarray(drawn.astype(out[name].dtype))
    for name, factor in factors.items():
        out[name] = (out[name] * factor).astype(out[name].dtype)
    return out
```

```python
import struct
from contextlib import ExitStack

import concourse.bass as bass
from concourse import mybir

F32 = mybir.dt.float32
BF16 = mybir.dt.bfloat16
I32 = mybir.dt.int32
ALU = mybir.AluOpType
ACT = mybir.ActivationFunctionType
AX = mybir.AxisListType

NODES, C, EDGES = 6250, 256, 100000
P = 125
NW = NODES // P
NPAIR = NW // 2
EP, EC = 125, EDGES // 125
GH = C // 4
HID = 4 * C
HC = HID // 128
KEEP = NODES // 2 - 1
EPS = 1e-5
TILE = 128
COLS = 1024
LOGF = 10
NB = 16
TILES = 832
NOH = NB
HCH = 200
NHIST = EC // HCH
COLBITS, ROWBITS = 13, 7
NOROW, NOWIN, BASE = 127, 63, 0x20000000
EMPTY = struct.unpack("<f", struct.pack("<I", BASE | NOWIN << COLBITS + ROWBITS | NOROW << COLBITS))[0]
PART = 3 * C
NEWTON = 3


def gps_layer(nc, x, src, dst, W, bias, Wqkv, Wproj, bproj, ln_g, ln_b, Wg1, bg1, Wg2, bg2,
              wr, br, w1, b1, w2, b2, out):
    table = nc.dram_tensor("table", (NODES, PART), BF16, kind="Internal").ap()
    ctx = ExitStack()
    with ctx:
        def sb(name, shape, dt=F32):
            return ctx.enter_context(nc.sbuf_tensor(name, shape, dt))

        def sem(name):
            return ctx.enter_context(nc.semaphore(name))

        bank = [ctx.enter_context(nc.psum_tensor(f"bank{i}", [128, 512], F32)) for i in range(8)]

        big_t = sb("big_t", [128, NW, C])
        big_g = sb("big_g", [P, NW, C])
        xnT = big_t[:, :, 0:2 * P].rearrange("p w (c n) -> p w c n", c=2)
        y_all = big_t[0:P, :, :]
        hot_row = big_t[0:EP, :, :].rearrange("p w c -> p (w c)").bitcast(BF16)[:, 0:P * HCH] \
            .rearrange("p (r j) -> p r j", j=HCH)
        keyA = sb("keyA", [128, COLS])
        keyB = sb("keyB", [128, COLS])
        col_of = sb("col_of", [128, COLS], I32)
        row_of = sb("row_of", [128, COLS])
        e_int = keyB[0:EP, 0:EC].bitcast(I32)
        gath = sb("gath", [128, NB, PART], BF16)
        gath_flat = gath[0:EP, :, :].rearrange("p s c -> p (s c)")
        hot_win = gath_flat[:, 0:NW * HCH].rearrange("p (w j) -> p w j", j=HCH)
        onehot = sb("onehot", [128, NOH, 128], BF16)
        idx_stage = sb("idx_stage", [128, NB], I32)
        sorted_keys = keyA
        row_b = onehot[0:EP, :, :].rearrange("p a b -> p (a b)")[:, 0:EC]
        win_b = onehot[0:EP, :, :].rearrange("p a b -> p (a b)")[:, 1024:1024 + EC]
        spent_all = onehot[:, :, :].rearrange("p a b -> p (a b)").bitcast(F32)
        iota_i = row_of[:, 0:128].bitcast(I32)
        iota_f = sb("iota_f", [128, 128])
        iota_b = sb("iota_b", [128, 128], BF16)
        part_i = sb("part_i", [128, 1], I32)
        part_f = sb("part_f", [128, 1])
        sign_i = sb("sign_i", [128, 8], I32)
        sign_t = sb("sign_t", [128, 8], I32)
        sign = sb("sign", [128, 8])
        ident = sb("ident", [128, 128])
        ident_b = sb("ident_b", [128, 128], BF16)
        lower = sb("lower", [128, 128])
        heads = sb("heads", [128, 128])
        ones = sb("ones", [128, 256])
        zeros_b = sb("zeros_b", [128, 264], BF16)
        zeros = zeros_b[:, :].bitcast(F32)
        W_in = sb("W_in", [128, 2, C])
        WT = sb("WT", [128, 2, C])
        qkv = sb("qkv", [128, 2, 3 * C])
        WqT = sb("WqT", [128, 2, C])
        Wqc = sb("Wqc", [128, 2, C])
        proj = sb("proj", [128, 2, C])
        Wg1_in = sb("Wg1_in", [128, 2, GH])
        Wg1_g = sb("Wg1_g", [128, 2, GH])
        Wg2_b = sb("Wg2_b", [GH + 1, C])
        w1_sb = sb("w1_sb", [128, 2, HID])
        w2_sb = sb("w2_sb", [128, HC, C])
        lng = sb("lng", [128, 2])
        lnb = sb("lnb", [128, 2])
        lnb_wide = sb("lnb_wide", [128, 2, 128])
        b1_sb = sb("b1_sb", [128, HC])
        bias_row = sb("bias_row", [1, C])
        bg1_bc = sb("bg1_bc", [P, GH])
        bproj_bc = sb("bproj_bc", [P, C])
        b2_bc = sb("b2_bc", [P, C])
        wr_bc = sb("wr_bc", [P, C])
        br_bc = sb("br_bc", [P, 1])
        bn = sb("bn", [P, 2, 6])
        mv = sb("mv", [P, NW, 2])
        rstd = sb("rstd", [P, NW])
        nmr = sb("nmr", [P, NW])
        r2 = sb("r2", [P, NW])
        deg = sb("deg", [P, NW])
        norm = sb("norm", [P, NW])
        nwt = sb("nwt", [P, 3, NW])
        cnt = spent_all[:, 0 * NW:1 * NW]
        til = spent_all[:, 1 * NW:2 * NW]
        til_i = spent_all[:, 2 * NW:3 * NW].bitcast(I32)
        pad = spent_all[:, 3 * NW:4 * NW]
        pad_i = spent_all[:, 4 * NW:5 * NW].bitcast(I32)
        scan = spent_all[:, 5 * NW:6 * NW]
        tile_end = sb("tile_end", [1, NW + 2], I32)
        xn = sb("xn", [P, 2, C])
        xT = sb("xT", [128, 2, 2, P])
        h_s = sb("h_s", [P, 2, C])
        h_res = sb("h_res", [P, 2, C])
        parts = sb("parts", [P, 2, 3, C], BF16)
        hg = sb("hg", [P, 2, GH])
        hgb = sb("hgb", [P, 2, GH])
        hact = sb("hact", [P, 2, GH])
        hgT = sb("hgT", [GH + 1, 2, P])
        kmax = sb("kmax", [128, 2])
        kmax2 = sb("kmax2", [128, 2])
        nkmax = sb("nkmax", [1, C])
        ek = xn
        vv_all = sb("vv", [128, 2, 2, 129])
        vv = vv_all[0:P, :, :, :]
        rden = sb("rden", [128, 2])
        ctxn = lnb_wide
        xt = h_s
        hself = parts[:, :, :, :].rearrange("p j a c -> p j (a c)")
        og = h_res
        ogT = W_in[:, 1, 0:2 * P].rearrange("p (c n) -> p c n", c=2)
        xb = W_in[0:P, 0, :]
        xm = keyA[0:P, 0 * C:1 * C]
        wz1 = sb("wz1", [P, 1])
        x1 = keyA[0:P, 1 * C:2 * C]
        z = keyA[0:P, 2 * C:3 * C]
        zw = keyA[0:P, 3 * C:4 * C]
        zT = vv_all[:, :, :, :].rearrange("p a b n -> p (a b n)")[:, 0:2 * P].rearrange("p (c n) -> p c n", c=2)
        hid = keyB[:, 0:HC * P].rearrange("p (k n) -> p k n", k=HC)
        mv2 = sb("mv2", [P, 2])
        rs2 = sb("rs2", [P, 3])
        wz = sb("wz", [P, NW])
        spent = spent_all[0:P, :]
        sel_i = spent[:, 0:NW].bitcast(I32)
        sel_m = spent[:, NW:2 * NW].bitcast(I32)
        half_k = spent[:, 2 * NW:4 * NW].rearrange("p (a w) -> p a w", a=2)
        mask = spent[:, 4 * NW:7 * NW].rearrange("p (a w) -> p a w", a=3)
        scr = spent[:, 7 * NW:8 * NW]
        csum = sb("csum", [P, 1])
        eqsum = sb("eqsum", [P, 1])
        thr = sb("thr", [P, 2])
        want = sb("want", [P, 2])
        tmp1 = sb("tmp1", [P, 2])
        coef = spent[:, 8 * NW:9 * NW]

        names = ("edges wload xload const const2 wprep wtp wev hotr hist stats nwt bn bna bg1 kps cntp chain sortd keyp "
                 "tabs tabfree final issued outs xn tp xT main hgv hgb erf hact gtp ghT gps gate hev split hout xstore "
                 "kT kmaxd kmt kmr stage kv ekv ctxp ctxd ctxn wqcp wqcd idx oh arrived used selfused staged "
                 "op og otp ogT pp xb xm sum x1 st nt zed zwt ztp zT hp gelu yp yv base csum").split()
        s = {n: sem("s_" + n) for n in names}
        s_slot = [sem(f"s_slot{j}") for j in range(NB)]
        s_hself = [sem(f"s_hself{j}") for j in range(2)]
        s_xt = [sem(f"s_xt{j}") for j in range(2)]
        s_tab = [sem(f"s_tab{j}") for j in range(2)]
        block = ctx.enter_context(nc.Block())

        src_v = src.rearrange("(p j) -> p j", p=EP)
        dst_v = dst.rearrange("(p j) -> p j", p=EP)
        x_v = x.rearrange("(p w) c -> p w c", w=NW)
        out_v = out.rearrange("(p w) c -> p w c", w=NW)
        tab_v = table.rearrange("(p w) c -> p w c", w=NW)
        OUTW = 5

        @block.sync
        def _(sp):
            sp.dma_start(e_int, src_v).then_inc(s["edges"], 16)
            sp.dma_start(col_of[0:EP, 0:EC], dst_v).then_inc(s["edges"], 16)
            sp.dma_start(big_g[:, 0:25, :], x_v[:, 0:25, :]).then_inc(s["xload"], 16)
            sp.dma_start(big_g[:, 25:50, :], x_v[:, 25:50, :]).then_inc(s["xload"], 16)
            loads = [
                (W_in[:, :, :], W.rearrange("(o p) i -> p o i", p=128)),
                (qkv[:, :, :], Wqkv.rearrange("(c p) n -> p c n", p=128)),
                (proj[:, :, :], Wproj.rearrange("(c p) n -> p c n", p=128)),
                (Wg1_in[:, :, :], Wg1.rearrange("(c p) n -> p c n", p=128)),
                (Wg2_b[0:GH, :], Wg2),
                (Wg2_b[GH:GH + 1, :], bg2.rearrange("(a n) -> a n", a=1)),
                (w1_sb[:, :, :], w1.rearrange("(c p) n -> p c n", p=128)),
                (w2_sb[:, :, :], w2.rearrange("(c p) n -> p c n", p=128)),
                (bias_row[:, :], bias.rearrange("(a n) -> a n", a=1)),
                (bg1_bc[:, :], bg1.rearrange("(a n) -> a n", a=1).to_broadcast([P, GH])),
                (bproj_bc[:, :], bproj.rearrange("(a n) -> a n", a=1).to_broadcast([P, C])),
                (b2_bc[:, :], b2.rearrange("(a n) -> a n", a=1).to_broadcast([P, C])),
                (wr_bc[:, :], wr.rearrange("n a -> a n").to_broadcast([P, C])),
                (br_bc[:, :], br.rearrange("(a n) -> a n", a=1).to_broadcast([P, 1])),
            ]
            for to, of in loads:
                sp.dma_start(to, of).then_inc(s["wload"], 16)
            with nc.allow_non_contiguous_dma(reason="three short vectors onto partitions"):
                sp.dma_start(lng[:, :], ln_g.rearrange("(c p) -> p c", p=128)).then_inc(s["wload"], 16)
                sp.dma_start(lnb[:, :], ln_b.rearrange("(c p) -> p c", p=128)).then_inc(s["wload"], 16)
                sp.dma_start(b1_sb[:, :], b1.rearrange("(c p) -> p c", p=128)).then_inc(s["wload"], 16)
            sp.sem_inc(s["tabfree"], 2)
            with sp.Fori(0, NPAIR) as i:
                for j in range(2):
                    sp.wait_ge(s["split"], i * 2 + (j + 3))
                    sp.dma_start(tab_v[:, bass.ds(i * 2 + j, 1), :].rearrange("p a c -> p (a c)"),
                                 parts[:, j, :, :].rearrange("p a c -> p (a c)")).then_inc(s_tab[j], 16)
                for j in range(2):
                    sp.wait_ge(s_tab[j], i * 16 + 16)
                    sp.sem_inc(s["tabfree"], 1)
            with sp.Fori(0, TILES // NB) as i:
                for j in range(NB):
                    sp.wait_ge(s_slot[j], i * 16 + 16)
                    sp.sem_inc(s["arrived"], 1)
            for g in range(NW // OUTW):
                sp.wait_ge(s["final"], (g + 1) * OUTW)
                sp.dma_start(out_v[:, g * OUTW:(g + 1) * OUTW, :],
                             big_g[:, g * OUTW:(g + 1) * OUTW, :]).then_inc(s["outs"], 16)
            sp.wait_ge(s["outs"], 16 * (NW // OUTW))

        @block.gpsimd
        def _(g):
            g.iota(iota_i[:, :], pattern=[[1, 128]], base=0, channel_multiplier=0).then_inc(s["const"], 1)
            g.iota(part_i[:, :], pattern=[[0, 1]], base=0, channel_multiplier=1).then_inc(s["const"], 1)
            g.memset(ident[:, :], 0.0).then_inc(s["const"], 1)
            g.memset(ones[:, :], 1.0).then_inc(s["const"], 1)
            g.memset(zeros[:, :], 0.0).then_inc(s["const"], 1)
            g.memset(vv_all[:, :, :, 128:129], 1.0).then_inc(s["const"], 1)
            g.wait_ge(s["const"], 6)
            g.affine_select(out=ident[:, :], in_=ident[:, :], compare_op=ALU.not_equal, fill=1.0, base=0,
                            pattern=[[-1, 128]], channel_multiplier=1).then_inc(s["const2"], 1)
            g.affine_select(out=lower[:, :], in_=ones[:, 0:128], compare_op=ALU.is_gt, fill=0.0, base=0,
                            pattern=[[1, 128]], channel_multiplier=-1).then_inc(s["const2"], 1)
            g.affine_select(out=heads[:, :], in_=ones[:, 0:128], compare_op=ALU.is_ge, fill=0.0, base=0,
                            pattern=[[-32, 4], [0, 32]], channel_multiplier=1).then_inc(s["const2"], 1)
            g.wait_ge(s["const2"], 3)
            g.affine_select(out=heads[:, :], in_=heads[:, :], compare_op=ALU.is_ge, fill=0.0, base=31,
                            pattern=[[32, 4], [0, 32]], channel_multiplier=-1).then_inc(s["const2"], 1)
            g.tensor_copy(ident_b[:, :], ident[:, :]).then_inc(s["const2"], 1)
            g.sem_inc(s["xstore"], 2)
            g.sem_inc(s["split"], 2)
            g.wait_ge(s["bg1"], 1)
            with g.Fori(0, NPAIR) as i:
                for j in range(2):
                    n = i * 2 + j + 1
                    g.wait_ge(s["hgv"], n)
                    g.sem_inc(s["issued"], 1)
                    g.tensor_tensor(hgb[:, j, :], hg[:, j, :], bg1_bc[:, :], ALU.add).then_inc(s["hgb"], 1)
                for j in range(2):
                    n = i * 2 + j + 1
                    g.wait_ge(s["xT"], n + 2)
                    g.sem_inc(s["issued"], 1)
                    g.tensor_copy(xnT[:, bass.ds(i * 2 + j, 1), :, :].rearrange("p a c n -> p (a c) n"),
                                  xT[:, j, :, :]).then_inc(s["xstore"], 1)
                    g.wait_ge(s["tabfree"], n)
                    g.sem_inc(s["issued"], 1)
                    g.wait_ge(s["hev"], n + 2)
                    g.sem_inc(s["issued"], 1)
                    g.tensor_copy(parts[:, j, 0, :], h_s[:, j, :]).then_inc(s["hout"], 1)
                    g.wait_ge(s["hout"], (i * 2 + j) * 3 + 1)
                    g.sem_inc(s["issued"], 1)
                    g.tensor_tensor(h_res[:, j, :], h_s[:, j, :], parts[:, j, 0, :], ALU.subtract).then_inc(s["hout"], 1)
                    g.wait_ge(s["hout"], (i * 2 + j) * 3 + 2)
                    g.sem_inc(s["issued"], 1)
                    g.tensor_copy(parts[:, j, 1, :], h_res[:, j, :]).then_inc(s["hout"], 1)
                    g.wait_ge(s["hout"], (i * 2 + j) * 3 + 3)
                    g.sem_inc(s["issued"], 1)
                    g.tensor_tensor(parts[:, j, 2, :], h_res[:, j, :], parts[:, j, 1, :], ALU.subtract).then_inc(s["split"], 1)
            g.wait_ge(s["xstore"], NW + 2)
            g.wait_ge(s["kT"], NW)
            with g.Fori(0, NPAIR) as i:
                for j in range(2):
                    g.wait_ge(s["kv"], i * 2 + j + 1)
                    g.sem_inc(s["issued"], 1)
                    g.tensor_copy(xT[:, j, :, :],
                                  xnT[:, bass.ds(i * 2 + j, 1), :, :].rearrange("p a c n -> p (a c) n")).then_inc(s["stage"], 1)
            for j in range(2):
                g.wait_ge(s_tab[j], 16 * NPAIR)
            g.wait_ge(s["tabs"], 1)
            last_row = g.to_reg(NODES - 1)
            with g.Fori(0, TILES // NB) as i:
                for half in range(2):
                    lo = half * (NB // 2)
                    g.wait_ge(s["used"], i * NB + (lo + NB // 2))
                    g.sem_inc(s["issued"], 1)
                    g.tensor_copy(idx_stage[:, lo:lo + NB // 2],
                                  col_of[:, bass.ds(i * NB + lo, NB // 2)]).then_inc(s["idx"], 1)
                    g.wait_ge(s["idx"], i * 2 + (half + 1))
                    g.sem_inc(s["issued"], 1)
                    for j in range(lo, lo + NB // 2):
                        g.wait_ge(s["used"], i * NB + (j + 1))
                        g.sem_inc(s["issued"], 1)
                        g.indirect_dma_start(
                            out=gath[:, j, :], out_offset=None, in_=table[:, :],
                            in_offset=bass.IndirectOffsetOnAxis(ap=idx_stage[:, j:j + 1], axis=0),
                            bounds_check=last_row, oob_is_err=True).then_inc(s_slot[j], 16)

        @block.scalar
        def _(a):
            for n, free in (("xT", 2), ("hev", 2), ("gate", 2), ("ekv", 4), ("ogT", 1), ("zT", 1), ("gelu", 1)):
                a.sem_inc(s[n], free)
            a.wait_ge(s["wload"], 16 * 17)
            for c in range(2):
                a.activation(Wg1_g[:, c, :], Wg1_in[:, c, :], ACT.Identity, scale=lng[:, c:c + 1]).then_inc(s["wev"], 1)
            a.wait_ge(s["wtp"], 1)
            a.activation(WT[:, :, :], bank[0][:, :].rearrange("p (c n) -> p c n", c=2), ACT.Copy).then_inc(s["wev"], 1)
            a.activation(WqT[:, :, :], bank[1][:, :].rearrange("p (c n) -> p c n", c=2), ACT.Copy).then_inc(s["wev"], 1)
            a.wait_ge(s["stats"], 1)
            with a.Fori(0, NPAIR) as i:
                for j in range(2):
                    w = i * 2 + j
                    a.wait_ge(s["tp"], w + 1)
                    a.sem_inc(s["issued"], 1)
                    a.activation(xn[:, j, :], big_g[:, bass.ds(w, 1), :].rearrange("p a c -> p (a c)"), ACT.Identity,
                                 bias=nmr[:, bass.ds(w, 1)], scale=rstd[:, bass.ds(w, 1)]).then_inc(s["xn"], 1)
                for j in range(2):
                    w = i * 2 + j
                    a.wait_ge(s["tp"], w + 3)
                    a.wait_ge(s["main"], w + 1)
                    a.wait_ge(s["xstore"], w + 1)
                    a.activation(xT[:, j, :, :], bank[j][:, 0:2 * P].rearrange("p (c n) -> p c n", c=2),
                                 ACT.Copy).then_inc(s["xT"], 1)
                for j in range(2):
                    w = i * 2 + j
                    a.wait_ge(s["main"], w + 3)
                    a.sem_inc(s["issued"], 1)
                    a.activation(hg[:, j, :], bank[2 + j][0:P, 256:256 + GH], ACT.Identity,
                                 scale=r2[:, bass.ds(w, 1)]).then_inc(s["hgv"], 1)
                    a.wait_ge(s["split"], w + 1)
                    a.sem_inc(s["issued"], 1)
                    a.activation(h_s[:, j, :], bank[2 + j][0:P, 0:C], ACT.Identity,
                                 scale=norm[:, bass.ds(w, 1)]).then_inc(s["hev"], 1)
                for j in range(2):
                    w = i * 2 + j
                    a.wait_ge(s["hgb"], w + 1)
                    a.activation(hact[:, j, :], hgb[:, j, :], ACT.Gelu).then_inc(s["hact"], 1)
                for j in range(2):
                    w = i * 2 + j
                    a.wait_ge(s["gtp"], w + 1)
                    a.activation(hgT[0:GH, j, :], bank[5][0:GH, j * 128:j * 128 + P], ACT.Copy).then_inc(s["ghT"], 1)
                for j in range(2):
                    w = i * 2 + j
                    a.wait_ge(s["gps"], w + 1)
                    a.sem_inc(s["issued"], 1)
                    a.activation(big_g[:, bass.ds(w, 1), :].rearrange("p a c -> p (a c)"),
                                 bank[6 + j][0:P, 0:C], ACT.Tanh, scale=0.5).then_inc(s["gate"], 1)
            a.wait_ge(s["kmt"], 1)
            a.activation(nkmax[:, :], bank[0][0:1, 0:C], ACT.Copy, scale=-1.0).then_inc(s["kmr"], 1)
            with a.Fori(0, NPAIR) as i:
                for j in range(2):
                    w = i * 2 + j
                    a.wait_ge(s["kv"], w + 3)
                    a.wait_ge(s["ctxp"], w + 1)
                    a.activation(ek[:, j, :], bank[2 + j][0:P, 0:C], ACT.Exp).then_inc(s["ekv"], 1)
                    a.activation(vv[:, j, :, 0:128], bank[2 + j][0:P, C:2 * C].rearrange("p (h n) -> p h n", h=2),
                                 ACT.Copy).then_inc(s["ekv"], 1)
            a.wait_ge(s["wqcd"], 1)
            for j in range(2):
                a.wait_ge(s_tab[j], 16 * NPAIR)
            with a.Fori(0, NPAIR) as i:
                for j in range(2):
                    w = i * 2 + j
                    a.wait_ge(s["selfused"], w + 1)
                    a.dma_start(hself[:, j, :], tab_v[:, bass.ds(w, 1), :].rearrange("p a c -> p (a c)")).then_inc(s_hself[j], 16)
                    a.wait_ge(s["xm"], w + 1)
                    a.dma_start(xt[:, j, :], x_v[:, bass.ds(w, 1), :].rearrange("p a c -> p (a c)")).then_inc(s_xt[j], 16)
                    a.wait_ge(s["op"], w + 1)
                    a.sem_inc(s["issued"], 1)
                    a.activation(xT[:, 0, :, :], xnT[:, bass.ds(w, 1), :, :].rearrange("p a c n -> p (a c) n"),
                                 ACT.Copy).then_inc(s["staged"], 1)
                    a.wait_ge(s["otp"], w + 2)
                    a.activation(ogT[:, :, :], bank[2][:, 0:2 * P].rearrange("p (c n) -> p c n", c=2),
                                 ACT.Copy).then_inc(s["ogT"], 1)
                    a.wait_ge(s["ztp"], w + 2)
                    a.activation(zT[:, :, :], bank[4][:, 0:2 * P].rearrange("p (c n) -> p c n", c=2),
                                 ACT.Copy).then_inc(s["zT"], 1)
                    for k in range(HC):
                        if k % 4 == 0:
                            a.wait_ge(s["hp"], w * 2 + (k // 4 + 1))
                            a.wait_ge(s["yp"], w + 1)
                        a.activation(hid[:, k, :], bank[5 + k // 4][:, (k % 4) * P:(k % 4 + 1) * P], ACT.Gelu_apprx_tanh,
                                     bias=b1_sb[:, k:k + 1]).then_inc(s["gelu"], 1)

        @block.tensor
        def _(t):
            for n, free in (("tp", 2), ("main", 2), ("kv", 2), ("ctxp", 2), ("selfused", 2), ("used", NB), ("op", 1),
                            ("otp", 1), ("ztp", 1), ("yp", 1)):
                t.sem_inc(s[n], free)
            t.wait_ge(s["wload"], 16 * 17)
            t.wait_ge(s["const2"], 5)
            for c in range(2):
                for o in range(2):
                    t.transpose(bank[0][:, c * C + o * 128:c * C + (o + 1) * 128],
                                W_in[:, o, c * 128:(c + 1) * 128], ident[:, :])
            for c in range(2):
                for o in range(2):
                    last = t.transpose(bank[1][:, c * C + o * 128:c * C + (o + 1) * 128],
                                       qkv[:, o, c * 128:(c + 1) * 128], ident[:, :])
            last.then_inc(s["wtp"], 1)
            t.matmul(bank[3][0:P, 0:NW], ident_b[:, 0:P], zeros_b[:, 0:NW], start=True, stop=False, skip_group_check=True)
            for n in range(NHIST):
                t.wait_ge(s["hotr"], n + 1)
                with t.Fori(0, HCH // 8) as i:
                    for u in range(8):
                        t.matmul(bank[3][0:P, 0:NW], hot_row[:, :, bass.ds(i * 8 + u, 1)].rearrange("p r a -> p (r a)"),
                                 hot_win[:, :, bass.ds(i * 8 + u, 1)].rearrange("p w a -> p (w a)"),
                                 start=False, stop=False, skip_group_check=True)
                t.matmul(bank[3][0:P, 0:NW], ident_b[:, 0:P], zeros_b[:, 0:NW], start=False, stop=n == NHIST - 1,
                         skip_group_check=True).then_inc(s["hist"], 1)
            t.wait_ge(s["wprep"], 1)
            for c in range(2):
                last = t.matmul(bank[2][0:P, 0:GH], lnb_wide[:, c, 0:P], Wg1_in[:, c, :], start=c == 0, stop=c == 1)
            last.then_inc(s["kps"], 1)
            t.wait_ge(s["nwt"], 1)
            t.matmul(bank[4][:, 0:NW], ones[0:P, 0:128], deg[:, :], start=True, stop=True).then_inc(s["cntp"], 1)
            t.wait_ge(s["wev"], 4)
            t.wait_ge(s["bg1"], 1)
            with t.Fori(0, NPAIR) as i:
                for j in range(2):
                    w = i * 2 + j
                    t.wait_ge(s["xn"], w + 1)
                    t.wait_ge(s["xT"], w + 1)
                    for c in range(2):
                        last = t.transpose(bank[j][:, c * P:(c + 1) * P], xn[:, j, c * 128:(c + 1) * 128], ident[0:P, 0:P])
                    last.then_inc(s["tp"], 1)
                for j in range(2):
                    w = i * 2 + j
                    t.wait_ge(s["xT"], w + 3)
                    t.wait_ge(s["hev"], w + 1)
                    for c in range(2):
                        t.matmul(bank[2 + j][0:P, C:C + GH], xT[:, j, c, :], Wg1_g[:, c, :], start=c == 0, stop=c == 1)
                    for c in range(2):
                        t.matmul(bank[2 + j][0:P, 0:C], xT[:, j, c, :], WT[:, c, :], start=c == 0, stop=False)
                    t.matmul(bank[2 + j][0:P, 0:C], ones[0:1, 0:P], bias_row[:, :], start=False, stop=True).then_inc(s["main"], 1)
                    if j == 0:
                        t.wait_ge(s["kmaxd"], i + 1)
                    for half in range(2):
                        for c in range(2):
                            last = t.matmul(bank[4][:, half * 256 + j * P:half * 256 + (j + 1) * P],
                                            qkv[:, c, C + half * 128:C + (half + 1) * 128], xT[:, j, c, :],
                                            start=c == 0, stop=c == 1)
                    last.then_inc(s["kT"], 1)
                for j in range(2):
                    w = i * 2 + j
                    t.wait_ge(s["hact"], w + 1)
                    t.sem_inc(s["issued"], 1)
                    t.transpose(bank[5][0:GH, j * 128:j * 128 + P], hact[:, j, :], ident[0:P, 0:P]).then_inc(s["gtp"], 1)
                    if j == 0:
                        t.wait_ge(s["ghT"], w + 1)
                for j in range(2):
                    w = i * 2 + j
                    t.wait_ge(s["ghT"], w + 1)
                    t.wait_ge(s["gate"], w + 1)
                    t.matmul(bank[6 + j][0:P, 0:C], hgT[:, j, :], Wg2_b[:, :], start=True, stop=True).then_inc(s["gps"], 1)
            t.wait_ge(s["kmaxd"], NPAIR + 1)
            t.wait_ge(s["gate"], NW + 2)
            for half in range(2):
                last = t.transpose(bank[0][0:1, half * 128:(half + 1) * 128], kmax[:, half:half + 1], ident[:, :])
            last.then_inc(s["kmt"], 1)
            for half in range(2):
                t.matmul(bank[6 + half][:, 0:129], ident[:, :], zeros[:, 0:129], start=True, stop=False, skip_group_check=True)
            t.wait_ge(s["kmr"], 1)
            with t.Fori(0, NPAIR) as i:
                for j in range(2):
                    w = i * 2 + j
                    t.wait_ge(s["stage"], w + 1)
                    t.wait_ge(s["ekv"], w * 2 + 2)
                    for c in range(2):
                        t.matmul(bank[2 + j][0:P, 0:C], xT[:, j, c, :], qkv[:, c, C:2 * C], start=c == 0, stop=False)
                    t.matmul(bank[2 + j][0:P, 0:C], ones[0:1, 0:P], nkmax[:, :], start=False, stop=True)
                    for c in range(2):
                        last = t.matmul(bank[2 + j][0:P, C:2 * C], xT[:, j, c, :], qkv[:, c, 2 * C:3 * C], start=c == 0, stop=c == 1)
                    last.then_inc(s["kv"], 1)
                for j in range(2):
                    w = i * 2 + j
                    t.wait_ge(s["ekv"], w * 2 + 6)
                    for half in range(2):
                        last = t.matmul(bank[6 + half][:, 0:129], ek[:, j, half * 128:(half + 1) * 128], vv[:, j, half, :],
                                        start=False, stop=False, skip_group_check=True)
                    last.then_inc(s["ctxp"], 1)
            for half in range(2):
                last = t.matmul(bank[6 + half][:, 0:129], ident[:, :], zeros[:, 0:129], start=False, stop=True, skip_group_check=True)
            last.then_inc(s["ctxd"], 1)
            t.wait_ge(s["sortd"], 1)
            for b in range(COLS // 128):
                last = t.transpose(bank[b // 4][:, (b % 4) * 128:(b % 4 + 1) * 128], sorted_keys[:, b * 128:(b + 1) * 128], ident[:, :])
            last.then_inc(s["keyp"], 1)
            t.wait_ge(s["ctxn"], 1)
            for c in range(2):
                for half in range(2):
                    last = t.matmul(bank[4][:, c * C + half * 128:c * C + (half + 1) * 128],
                                    WqT[:, half, c * 128:(c + 1) * 128], ctxn[:, half, :], start=True, stop=True)
            last.then_inc(s["wqcp"], 1)
            t.wait_ge(s["wqcd"], 1)
            t.wait_ge(s["tabs"], 2)
            with t.Fori(0, NPAIR) as i:
                for j in range(2):
                    w = i * 2 + j
                    t.wait_ge(s_hself[j], i * 16 + 16)
                    t.wait_ge(s["x1"], w + 1)
                    for k in range(3):
                        last = t.matmul(bank[0][0:P, 0:C], ident_b[0:P, 0:P], hself[:, j, k * C:(k + 1) * C],
                                        start=k == 0, stop=False, skip_group_check=True)
                    last.then_inc(s["selfused"], 1)
                    first = t.value_load(tile_end[0:1, bass.ds(w, 1)], min_val=0, max_val=TILES - 1)
                    end = t.value_load(tile_end[0:1, bass.ds(w + 1, 1)], min_val=1, max_val=TILES)
                    with t.Fori(first, end) as q:
                        t.wait_ge(s["oh"], q + 1)
                        t.wait_ge(s["arrived"], q + 1)
                        for k in range(3):
                            last = t.matmul(bank[0][0:P, 0:C], onehot[:, bass.ds(q % NOH, 1), 0:P].rearrange("p a r -> p (a r)"),
                                            gath[:, bass.ds(q % NB, 1), k * C:(k + 1) * C].rearrange("p a c -> p (a c)"),
                                            start=False, stop=False, skip_group_check=True)
                        last.then_inc(s["used"], 1)
                    t.matmul(bank[0][0:P, 0:C], ident_b[:, 0:P], zeros_b[:, 0:C], start=False, stop=True,
                             skip_group_check=True).then_inc(s["sum"], 1)
                    t.wait_ge(s["staged"], w + 1)
                    t.wait_ge(s["og"], w + 1)
                    for c in range(2):
                        last = t.matmul(bank[1][0:P, 0:C], xT[:, 0, c, :], Wqc[:, c, :], start=c == 0, stop=c == 1)
                    last.then_inc(s["op"], 1)
                    t.wait_ge(s["og"], w + 2)
                    t.wait_ge(s["ogT"], w + 1)
                    for c in range(2):
                        last = t.transpose(bank[2][:, c * P:(c + 1) * P], og[:, 0, c * 128:(c + 1) * 128], ident[0:P, 0:P])
                    last.then_inc(s["otp"], 1)
                    t.wait_ge(s["ogT"], w + 2)
                    t.wait_ge(s["xm"], w + 2)
                    for c in range(2):
                        last = t.matmul(bank[3][0:P, 0:C], ogT[:, c, :], proj[:, c, :], start=c == 0, stop=c == 1)
                    last.then_inc(s["pp"], 1)
                    t.wait_ge(s["zed"], w + 1)
                    t.wait_ge(s["zT"], w + 1)
                    for c in range(2):
                        last = t.transpose(bank[4][:, c * P:(c + 1) * P], z[:, c * 128:(c + 1) * 128], ident[0:P, 0:P])
                    last.then_inc(s["ztp"], 1)
                    t.wait_ge(s["zT"], w + 2)
                    t.wait_ge(s["gelu"], w * HC + 1)
                    for k in range(HC):
                        for c in range(2):
                            last = t.matmul(bank[5 + k // 4][:, (k % 4) * P:(k % 4 + 1) * P],
                                            w1_sb[:, c, k * 128:(k + 1) * 128], zT[:, c, :], start=c == 0, stop=c == 1)
                        if k % 4 == 3:
                            last.then_inc(s["hp"], 1)
                    t.wait_ge(s["yv"], w + 1)
                    for k in range(HC):
                        t.wait_ge(s["gelu"], w * HC + (k + 2))
                        last = t.matmul(bank[7][0:P, 0:C], hid[:, k, :], w2_sb[:, k, :], start=k == 0, stop=k == HC - 1)
                    last.then_inc(s["yp"], 1)
            for n in range(32):
                t.wait_ge(s["csum"], n + 1)
                t.matmul(bank[0][0:P, 0:1], ones[0:P, 0:P], csum[:, :], start=True, stop=True).then_inc(s["cntp"], 1)
            t.wait_ge(s["csum"], 33)
            t.matmul(bank[0][0:P, 0:1], ones[0:P, 0:P], csum[:, :], start=True, stop=True)
            t.matmul(bank[1][0:P, 0:1], lower[0:P, 0:P], eqsum[:, :], start=True, stop=True).then_inc(s["cntp"], 1)

        @block.vector
        def _(v):
            made = [0]

            def step(ins):
                made[0] += 1
                ins.then_inc(s["chain"], 1)
                v.wait_ge(s["chain"], made[0])

            v.wait_ge(s["const"], 6)
            step(nc.vector.memset(hgT[GH:GH + 1, :, :], 1.0))
            step(nc.vector.tensor_copy(iota_f[:, :], iota_i[:, :]))
            step(nc.vector.tensor_copy(iota_b[:, :], iota_f[:, :]))
            step(nc.vector.tensor_copy(part_f[:, :], part_i[:, :]))
            for m in range(8):
                step(nc.vector.tensor_scalar(sign_i[:, m:m + 1], part_i[:, :], max(m - 1, 0), None, ALU.logical_shift_right))
            for m in range(8):
                if m == 0:
                    step(nc.vector.tensor_copy(sign_t[:, m:m + 1], sign_i[:, m:m + 1]))
                else:
                    step(nc.vector.tensor_scalar(sign_t[:, m:m + 1], sign_i[:, m:m + 1], 1, None, ALU.logical_shift_right))
                    step(nc.vector.tensor_tensor(sign_t[:, m:m + 1], sign_t[:, m:m + 1], sign_i[:, m:m + 1], ALU.bitwise_xor))
            step(nc.vector.tensor_scalar(sign_t[:, :], sign_t[:, :], 1, None, ALU.bitwise_and))
            step(nc.vector.tensor_copy(sign[:, :], sign_t[:, :]))
            step(nc.vector.tensor_scalar(sign[:, :], sign[:, :], -2.0, 1.0, ALU.mult, ALU.add))
            v.wait_ge(s["edges"], 32)
            step(nc.vector.tensor_copy(keyA[0:EP, 0:EC], e_int))
            row_i = row_of[0:EP, 0:EC].bitcast(I32)
            step(nc.vector.tensor_scalar(row_i, keyA[0:EP, 0:EC], 1.0 / NW, -0.49, ALU.mult, ALU.add))
            step(nc.vector.tensor_copy(row_b, row_i))
            step(nc.vector.scalar_tensor_tensor(keyA[0:EP, 0:EC], row_i, -float(NW), keyA[0:EP, 0:EC], ALU.mult, ALU.add))
            step(nc.vector.tensor_copy(win_b, keyA[0:EP, 0:EC]))
            step(nc.vector.tensor_copy(e_int, keyA[0:EP, 0:EC]))

            def histogram(n):
                if n:
                    v.wait_ge(s["hist"], n)
                at = slice(n * HCH, (n + 1) * HCH)
                for w in range(NW):
                    nc.vector.tensor_scalar(hot_win[:, w, :], win_b[:, at], float(w), None, ALU.is_equal)
                for r in range(P):
                    last = nc.vector.tensor_scalar(hot_row[:, r, :], row_b[:, at], float(r), None, ALU.is_equal)
                last.then_inc(s["hotr"], 1)

            def node_stats(w):
                nc.vector.bn_stats(bn[:, w % 2, :], big_g[:, w, :]).then_inc(s["bn"], 1)
                v.wait_ge(s["bn"], w + 1)
                nc.vector.bn_aggr(mv[:, w, :], bn[:, w % 2, :]).then_inc(s["bna"], 1)

            def inverse_sqrt(to, of, t):
                step(nc.vector.tensor_scalar(t.bitcast(I32), of.bitcast(I32), 1, None, ALU.logical_shift_right))
                step(nc.vector.tensor_scalar(to.bitcast(I32), t.bitcast(I32), -1.0, float(0x5F3759DF), ALU.mult, ALU.add))
                for _ in range(NEWTON):
                    step(nc.vector.tensor_tensor(t, to, to, ALU.mult))
                    step(nc.vector.tensor_tensor(t, t, of, ALU.mult))
                    step(nc.vector.tensor_scalar(t, t, -0.5, 1.5, ALU.mult, ALU.add))
                    step(nc.vector.tensor_tensor(to, to, t, ALU.mult))

            histogram(0)
            step(nc.vector.memset(keyA[:, :], EMPTY))
            step(nc.vector.tensor_scalar(e_int, e_int, COLBITS + ROWBITS, BASE, ALU.logical_shift_left, ALU.bitwise_or))
            step(nc.vector.tensor_scalar(row_i, row_i, COLBITS, None, ALU.logical_shift_left))
            step(nc.vector.tensor_tensor(e_int, e_int, row_i, ALU.bitwise_or))
            step(nc.vector.tensor_tensor(keyA[0:EP, 0:EC].bitcast(I32), e_int, col_of[0:EP, 0:EC], ALU.bitwise_or))
            v.wait_ge(s["wload"], 16 * 17)
            for c in range(2):
                last = nc.vector.tensor_scalar(lnb_wide[:, c, :], ones[:, 0:128], lnb[:, c:c + 1], None, ALU.mult)
            last.then_inc(s["wprep"], 1)
            v.wait_ge(s["xload"], 32)
            for w in range(NW // 2):
                node_stats(w)
            histogram(1)
            for w in range(NW // 2, NW):
                node_stats(w)
            v.wait_ge(s["bna"], NW)
            step(nc.vector.tensor_scalar(nwt[:, 0, :], mv[:, :, 1], EPS, None, ALU.add))
            inverse_sqrt(rstd[:, :], nwt[:, 0, :], nwt[:, 1, :])
            step(nc.vector.scalar_tensor_tensor(nmr[:, :], mv[:, :, 0], -1.0, rstd[:, :], ALU.mult, ALU.mult))
            step(nc.vector.tensor_tensor(nwt[:, 0, :], mv[:, :, 1], rstd[:, :], ALU.mult))
            step(nc.vector.tensor_tensor(nwt[:, 0, :], nwt[:, 0, :], rstd[:, :], ALU.mult))
            step(nc.vector.tensor_scalar(nwt[:, 0, :], nwt[:, 0, :], EPS, None, ALU.add))
            inverse_sqrt(r2[:, :], nwt[:, 0, :], nwt[:, 1, :])
            histogram(2)
            histogram(3)
            v.wait_ge(s["hist"], NHIST)
            nc.vector.tensor_copy(deg[:, :], bank[3][0:P, 0:NW]).then_inc(s["nwt"], 1)
            v.wait_ge(s["nwt"], 1)
            step(nc.vector.tensor_scalar(nwt[:, 0, :], deg[:, :], 1.0, None, ALU.add))
            inverse_sqrt(norm[:, :], nwt[:, 0, :], nwt[:, 1, :])
            nc.vector.memset(kmax[:, :], -3.0e38).then_inc(s["stats"], 1)
            v.wait_ge(s["kps"], 1)
            nc.vector.tensor_tensor(bg1_bc[:, :], bank[2][0:P, 0:GH], bg1_bc[:, :], ALU.add).then_inc(s["bg1"], 1)
            v.wait_ge(s["cntp"], 1)
            nc.vector.tensor_copy(cnt[:, :], bank[4][:, 0:NW]).then_inc(s["kmaxd"], 1)
            v.wait_ge(s["kmaxd"], 1)
            step(nc.vector.tensor_scalar(til_i[:, :], cnt[:, :], 1.0 / TILE, 127.0 / TILE - 0.49609375, ALU.mult, ALU.add))
            step(nc.vector.tensor_scalar(til[:, :], til_i[:, :], 1.0, None, ALU.max))
            step(nc.vector.scalar_tensor_tensor(pad[:, :], til[:, :], float(TILE), cnt[:, :], ALU.mult, ALU.subtract))
            step(nc.vector.tensor_scalar(pad[:, :], pad[:, :], part_f[:, :], None, ALU.is_gt))
            step(nc.vector.tensor_scalar(cnt[:, :], iota_f[:, 0:NW], -float(NOWIN), None, ALU.add))
            step(nc.vector.tensor_tensor(pad[:, :], pad[:, :], cnt[:, :], ALU.mult))
            step(nc.vector.tensor_scalar(pad_i[:, :], pad[:, :], float(NOWIN), None, ALU.add))
            step(nc.vector.tensor_scalar(keyA[:, EC:EC + NW].bitcast(I32), pad_i[:, :], COLBITS + ROWBITS,
                                         BASE | NOROW << COLBITS, ALU.logical_shift_left, ALU.bitwise_or))
            step(nc.vector.tensor_tensor_scan(scan[:, :], ones[:, 0:NW], til[:, :], 0.0, ALU.mult, ALU.add))
            step(nc.vector.memset(tile_end[:, :], 0))
            step(nc.vector.tensor_copy(tile_end[:, 1:NW], scan[0:1, 0:NW - 1]))
            step(nc.vector.memset(tile_end[:, NW:NW + 1], TILES))

            cur = [keyA, keyB]
            stages = [0]
            peeks = [0]

            def peek():
                n = peeks[0]
                if n < NPAIR and stages[0] % 5 == 0:
                    v.wait_ge(s["kT"], 2 * n + 2)
                    step(nc.vector.tensor_reduce(kmax2[:, :], bank[4][:, :].rearrange("p (h n) -> p h n", h=2)[:, :, 0:2 * P],
                                                 AX.X, ALU.max))
                    nc.vector.tensor_tensor(kmax[:, :], kmax[:, :], kmax2[:, :], ALU.max).then_inc(s["kmaxd"], 1)
                    peeks[0] += 1

            def exchange(lo_in, hi_in, lo_out, hi_out):
                nc.vector.tensor_tensor(lo_out, lo_in, hi_in, ALU.min).then_inc(s["chain"], 1)
                nc.vector.tensor_tensor(hi_out, lo_in, hi_in, ALU.max).then_inc(s["chain"], 1)
                made[0] += 2
                v.wait_ge(s["chain"], made[0])
                cur.reverse()
                stages[0] += 1
                peek()

            def distance(d):
                a, b = (k[:, :].rearrange("p (n two d) -> p n two d", two=2, d=d) for k in cur)
                exchange(a[:, :, 0, :], a[:, :, 1, :], b[:, :, 0, :], b[:, :, 1, :])

            def swap_blocks():
                step(nc.vector.transpose(cur[1][:, :], cur[0][:, :]))
                cur.reverse()

            def turn(m):
                step(nc.vector.tensor_scalar(cur[0][:, :], cur[0][:, :], sign[:, m:m + 1], None, ALU.mult))

            turn(0)
            for k in range(1, LOGF + 1):
                size = 1 << k
                a, b = (q[:, :].rearrange("p (n s) -> p n s", s=size) for q in cur)
                hi = a[:, :, size - 1:size // 2 - 1:-1] if size > 2 else a[:, :, 1:2]
                exchange(a[:, :, 0:size // 2], hi, b[:, :, 0:size // 2], b[:, :, size // 2:size])
                for e in range(k - 2, -1, -1):
                    distance(1 << e)
            for m in range(1, 8):
                turn(m)
                if m >= 7:
                    a, b = cur
                    step(nc.vector.tensor_tensor(b[0:64, :], a[0:64, :], a[64:128, :], ALU.min))
                    step(nc.vector.tensor_tensor(b[64:128, :], a[0:64, :], a[64:128, :], ALU.max))
                    cur.reverse()
                if m >= 6:
                    a, b = cur
                    for q in (0, 64):
                        step(nc.vector.tensor_tensor(b[q:q + 32, :], a[q:q + 32, :], a[q + 32:q + 64, :], ALU.min))
                        step(nc.vector.tensor_tensor(b[q + 32:q + 64, :], a[q:q + 32, :], a[q + 32:q + 64, :], ALU.max))
                    cur.reverse()
                swap_blocks()
                for e in range(min(m, 5) - 1, -1, -1):
                    distance(1 << e)
                swap_blocks()
                for e in range(LOGF - 1, 6 if m == 7 else -1, -1):
                    distance(1 << e)
            while peeks[0] < NPAIR:
                stages[0] = 0
                peek()
            v.wait_ge(s["kmaxd"], NPAIR + 1)
            assert cur[0] is sorted_keys
            v.sem_inc(s["sortd"], 1)
            v.wait_ge(s["keyp"], 1)
            spare = cur[1]
            for h in range(2):
                step(nc.vector.tensor_copy(spare[:, h * 512:(h + 1) * 512], bank[h][:, :]))
            keys_i = spare[:, :].bitcast(I32).rearrange("q (b p) -> q b p", b=8)
            nc.vector.tensor_scalar(col_of[:, :].rearrange("q (p b) -> q b p", b=8), keys_i, (1 << COLBITS) - 1, None,
                                    ALU.bitwise_and).then_inc(s["tabs"], 1)
            step(nc.vector.tensor_scalar(cur[0][:, :].bitcast(I32).rearrange("q (b p) -> q b p", b=8), keys_i, COLBITS,
                                         (1 << ROWBITS) - 1, ALU.logical_shift_right, ALU.bitwise_and))
            nc.vector.tensor_copy(row_of[:, :].rearrange("q (p b) -> q b p", b=8),
                                  cur[0][:, :].bitcast(I32).rearrange("q (b p) -> q b p", b=8)).then_inc(s["tabs"], 1)
            v.wait_ge(s["ctxd"], 1)
            for half in range(2):
                step(nc.vector.reciprocal(rden[:, half:half + 1], bank[6 + half][:, 128:129]))
            for half in range(2):
                last = nc.vector.scalar_tensor_tensor(ctxn[:, half, :], bank[6 + half][:, 0:128], rden[:, half:half + 1],
                                                      heads[:, :], ALU.mult, ALU.mult)
                if half == 0:
                    step(last)
            last.then_inc(s["ctxn"], 1)
            v.wait_ge(s["wqcp"], 1)
            nc.vector.tensor_scalar(Wqc[:, :, :], bank[4][:, :].rearrange("p (c n) -> p c n", c=2), 0.5, None,
                                    ALU.mult).then_inc(s["wqcd"], 1)
            v.wait_ge(s["tabs"], 2)
            for n in ("x1", "og", "yv"):
                v.sem_inc(s[n], 1)
            v.sem_inc(s["xm"], 2)
            with v.Fori(0, NPAIR) as i:
                for j in range(2):
                    w = i * 2 + j
                    first = v.value_load(tile_end[0:1, bass.ds(w, 1)], min_val=0, max_val=TILES - 1)
                    end = v.value_load(tile_end[0:1, bass.ds(w + 1, 1)], min_val=1, max_val=TILES)
                    with v.Fori(first, end) as q:
                        v.wait_ge(s["used"], q + 1)
                        nc.vector.tensor_scalar(onehot[:, bass.ds(q % NOH, 1), 0:P].rearrange("p a r -> p (a r)"),
                                                iota_b[:, 0:P], row_of[:, bass.ds(q, 1)], None, ALU.is_equal).then_inc(s["oh"], 1)
                    wi = bass.ds(w, 1)
                    gate = big_g[:, wi, :].rearrange("p a c -> p (a c)")
                    v.wait_ge(s["op"], w + 2)
                    v.wait_ge(s["otp"], w + 1)
                    nc.vector.scalar_tensor_tensor(og[:, 0, :], gate, 1.0, bank[1][0:P, 0:C], ALU.add, ALU.mult).then_inc(s["og"], 1)
                    v.wait_ge(s_xt[j], i * 16 + 16)
                    nc.vector.tensor_tensor(xb[:, :], xt[:, j, :], bproj_bc[:, :], ALU.add).then_inc(s["xb"], 1)
                    v.wait_ge(s["xb"], w + 1)
                    v.wait_ge(s["pp"], w + 1)
                    nc.vector.tensor_tensor(xm[:, :], bank[3][0:P, 0:C], xb[:, :], ALU.add).then_inc(s["xm"], 1)
                    v.wait_ge(s["xm"], w + 3)
                    v.wait_ge(s["sum"], w + 1)
                    nc.vector.scalar_tensor_tensor(x1[:, :], bank[0][0:P, 0:C], norm[:, wi], xm[:, :],
                                                   ALU.mult, ALU.add).then_inc(s["x1"], 1)
                    v.wait_ge(s["x1"], w + 2)
                    nc.vector.bn_stats(bn[:, 0, :], x1[:, :]).then_inc(s["st"], 1)
                    v.wait_ge(s["st"], w * 2 + 1)
                    v.sem_inc(s["issued"], 1)
                    nc.vector.bn_aggr(mv2[:, :], bn[:, 0, :]).then_inc(s["st"], 1)
                    v.wait_ge(s["st"], w * 2 + 2)
                    per = 3 + 3 * NEWTON
                    var, root, t0 = rs2[:, 0:1], rs2[:, 1:2], rs2[:, 2:3]
                    ops = [lambda: nc.vector.tensor_scalar(var, mv2[:, 1:2], EPS, None, ALU.add),
                           lambda: nc.vector.tensor_scalar(t0.bitcast(I32), var.bitcast(I32), 1, None, ALU.logical_shift_right),
                           lambda: nc.vector.tensor_scalar(root.bitcast(I32), t0.bitcast(I32), -1.0, float(0x5F3759DF), ALU.mult, ALU.add)]
                    for _ in range(NEWTON):
                        ops += [lambda: nc.vector.tensor_scalar(t0, root, root, var, ALU.mult, ALU.mult),
                                lambda: nc.vector.tensor_scalar(t0, t0, -0.5, 1.5, ALU.mult, ALU.add),
                                lambda: nc.vector.tensor_tensor(root, root, t0, ALU.mult)]
                    assert len(ops) == per
                    for n, op in enumerate(ops):
                        op().then_inc(s["nt"], 1)
                        v.wait_ge(s["nt"], w * per + (n + 1))
                    v.wait_ge(s["ztp"], w + 1)
                    nc.vector.tensor_scalar(z[:, :], x1[:, :], mv2[:, 0:1], root, ALU.subtract, ALU.mult).then_inc(s["zed"], 1)
                    v.wait_ge(s["zed"], w + 1)
                    nc.vector.tensor_tensor_reduce(out=zw[:, :], in0=z[:, :], in1=wr_bc[:, :], scale=1.0, scalar=0.0,
                                                   op0=ALU.mult, op1=ALU.add, accum_out=wz1[:, :]).then_inc(s["zwt"], 1)
                    nc.vector.tensor_tensor(gate, x1[:, :], z[:, :], ALU.add).then_inc(s["base"], 1)
                    v.wait_ge(s["zwt"], w + 1)
                    nc.vector.tensor_tensor(wz[:, wi], wz1[:, :], br_bc[:, :], ALU.add).then_inc(s["base"], 1)
                    v.wait_ge(s["yp"], w + 2)
                    nc.vector.tensor_tensor(y_all[:, wi, :].rearrange("p a c -> p (a c)"), bank[7][0:P, 0:C], b2_bc[:, :],
                                            ALU.add).then_inc(s["yv"], 1)
            v.wait_ge(s["yv"], NW + 1)
            v.wait_ge(s["base"], 2 * NW)
            step(nc.vector.tensor_scalar(wz[:, :], wz[:, :], 0.0, None, ALU.add))
            wz_i = wz[:, :].bitcast(I32)
            step(nc.vector.tensor_scalar(sel_m[:, :], wz_i, 31, 1, ALU.arith_shift_right, ALU.logical_shift_right))
            step(nc.vector.tensor_tensor(sel_i[:, :], wz_i, sel_m[:, :], ALU.bitwise_xor))
            step(nc.vector.tensor_scalar(sel_m[:, :], sel_i[:, :], -0x80000000, None, ALU.bitwise_xor))
            step(nc.vector.tensor_scalar(sel_i[:, :], sel_m[:, :], 16, None, ALU.logical_shift_right))
            step(nc.vector.tensor_copy(half_k[:, 0, :], sel_i[:, :]))
            step(nc.vector.tensor_scalar(sel_i[:, :], sel_m[:, :], 0xFFFF, None, ALU.bitwise_and))
            step(nc.vector.tensor_copy(half_k[:, 1, :], sel_i[:, :]))
            step(nc.vector.memset(thr[:, :], 0.0))
            counts = 0
            for part in range(2):
                if part:
                    step(nc.vector.tensor_scalar(mask[:, 0, :], half_k[:, 0, :], thr[:, 0:1], None, ALU.is_gt))
                    step(nc.vector.tensor_scalar(mask[:, 1, :], half_k[:, 0, :], thr[:, 0:1], None, ALU.is_equal))
                    step(nc.vector.scalar_tensor_tensor(half_k[:, 1, :], half_k[:, 1, :], 1.0, mask[:, 1, :], ALU.add, ALU.mult))
                    step(nc.vector.scalar_tensor_tensor(half_k[:, 1, :], mask[:, 0, :], 131072.0, half_k[:, 1, :], ALU.mult, ALU.add))
                    step(nc.vector.memset(thr[:, 1:2], 1.0))
                for bit in range(15, -1, -1):
                    step(nc.vector.tensor_scalar(tmp1[:, 0:1], thr[:, part:part + 1], float(1 << bit), None, ALU.add))
                    nc.vector.tensor_scalar(scr[:, :], half_k[:, part, :], tmp1[:, 0:1], None, ALU.is_ge, ALU.add,
                                            accum_out=csum[:, :]).then_inc(s["csum"], 1)
                    counts += 1
                    v.wait_ge(s["cntp"], 1 + counts)
                    step(nc.vector.tensor_scalar(tmp1[:, 1:2], bank[0][0:P, 0:1], float(KEEP), float(1 << bit), ALU.is_ge, ALU.mult))
                    step(nc.vector.tensor_tensor(thr[:, part:part + 1], thr[:, part:part + 1], tmp1[:, 1:2], ALU.add))
            step(nc.vector.tensor_scalar(mask[:, 1, :], half_k[:, 1, :], thr[:, 1:2], None, ALU.is_equal, ALU.add, accum_out=eqsum[:, :]))
            nc.vector.tensor_scalar(mask[:, 0, :], half_k[:, 1, :], thr[:, 1:2], None, ALU.is_gt, ALU.add,
                                    accum_out=csum[:, :]).then_inc(s["csum"], 1)
            step(nc.vector.tensor_tensor_scan(mask[:, 2, :], ones[0:P, 0:NW], mask[:, 1, :], 0.0, ALU.mult, ALU.add))
            v.wait_ge(s["cntp"], 34)
            step(nc.vector.tensor_scalar(tmp1[:, 0:1], bank[0][0:P, 0:1], -1.0, float(KEEP), ALU.mult, ALU.add))
            step(nc.vector.tensor_scalar(tmp1[:, 1:2], bank[1][0:P, 0:1], tmp1[:, 0:1], -1.0, ALU.subtract, ALU.mult))
            step(nc.vector.tensor_scalar(mask[:, 2, :], mask[:, 2, :], tmp1[:, 1:2], None, ALU.is_le))
            step(nc.vector.tensor_tensor(mask[:, 1, :], mask[:, 1, :], mask[:, 2, :], ALU.mult))
            step(nc.vector.tensor_tensor(mask[:, 0, :], mask[:, 0, :], mask[:, 1, :], ALU.add))
            step(nc.vector.tensor_tensor(coef[:, :], mask[:, 0, :], wz[:, :], ALU.mult))
            for w in range(NW):
                nc.vector.scalar_tensor_tensor(big_g[:, w, :], y_all[:, w, :], coef[:, w:w + 1], big_g[:, w, :],
                                               ALU.mult, ALU.add).then_inc(s["final"], 1)


_INS = ["x", "src", "dst", "L0_gnn_W", "L0_gnn_bias", "L0_mix_Wqkv", "L0_mix_Wproj", "L0_mix_bproj", "L0_mix_ln_g",
        "L0_mix_ln_b", "L0_mix_Wg1", "L0_mix_bg1", "L0_mix_Wg2", "L0_mix_bg2", "L0_ffn_wr", "L0_ffn_br",
        "L0_ffn_w1", "L0_ffn_b1", "L0_ffn_w2", "L0_ffn_b2"]


def kernel(**inputs):
    import numpy as _np
    import concourse.bacc as _bacc
    from concourse import mybir as _mybir
    from concourse.bass_utils import run_bass_kernel_spmd as _run

    nc = _bacc.Bacc("TRN2", target_bir_lowering=False, num_devices=1)
    arrays, args = {}, []
    for name in _INS:
        a = _np.ascontiguousarray(inputs[name])
        arrays[f"in_{name}"] = a
        args.append(nc.dram_tensor(f"in_{name}", a.shape, _mybir.dt.from_np(a.dtype), kind="ExternalInput").ap())
    args.append(nc.dram_tensor("out_0", (NODES, C), _mybir.dt.float32, kind="ExternalOutput").ap())
    gps_layer(nc, *args)
    r = _run(nc, [arrays], core_ids=[0])
    return r.results[0]["out_0"]
```

```python
import struct
from contextlib import ExitStack

import concourse.bass as bass
from concourse import mybir

F32 = mybir.dt.float32
BF16 = mybir.dt.bfloat16
I32 = mybir.dt.int32
ALU = mybir.AluOpType
ACT = mybir.ActivationFunctionType
AX = mybir.AxisListType

NODES, C, EDGES = 6250, 256, 100000
P = 125
NW = NODES // P
NPAIR = NW // 2
EP, EC = 125, EDGES // 125
GH = C // 4
HID = 4 * C
HC = HID // 128
KEEP = NODES // 2 - 1
EPS = 1e-5
TILE = 128
COLS = 1024
LOGF = 10
NB = 16
GROUP = 4
GEDGE = GROUP * TILE
ROUND = NB // GROUP
NOH = NB

MAXG = COLS // GROUP
HCH = 200
NHIST = EC // HCH
COLBITS, ROWBITS = 13, 7
NOROW, NOWIN, BASE = 127, 63, 0x20000000
EMPTY = struct.unpack("<f", struct.pack("<I", BASE | NOWIN << COLBITS + ROWBITS | NOROW << COLBITS))[0]
PART = 3 * C
NEWTON = 3


def gps_layer(nc, x, src, dst, W, bias, Wqkv, Wproj, bproj, ln_g, ln_b, Wg1, bg1, Wg2, bg2,
              wr, br, w1, b1, w2, b2, out):
    table = nc.dram_tensor("table", (NODES, PART), BF16, kind="Internal").ap()
    ctx = ExitStack()
    with ctx:
        def sb(name, shape, dt=F32):
            return ctx.enter_context(nc.sbuf_tensor(name, shape, dt))

        def sem(name):
            return ctx.enter_context(nc.semaphore(name))

        bank = [ctx.enter_context(nc.psum_tensor(f"bank{i}", [128, 512], F32)) for i in range(8)]

        big_t = sb("big_t", [128, NW, C])
        big_g = sb("big_g", [P, NW, C])
        xnT = big_t[:, :, 0:2 * P].rearrange("p w (c n) -> p w c n", c=2)
        y_all = big_t[0:P, :, :]
        hot_row = big_t[0:EP, :, :].rearrange("p w c -> p (w c)").bitcast(BF16)[:, 0:P * HCH] \
            .rearrange("p (r j) -> p r j", j=HCH)
        keyA = sb("keyA", [128, COLS])
        keyB = sb("keyB", [128, COLS])
        col_of = sb("col_of", [128, COLS], I32)
        row_of = sb("row_of", [128, COLS])
        e_int = keyB[0:EP, 0:EC].bitcast(I32)
        gath = sb("gath", [128, NB, PART], BF16)
        gath_flat = gath[0:EP, :, :].rearrange("p s c -> p (s c)")
        hot_win = gath_flat[:, 0:NW * HCH].rearrange("p (w j) -> p w j", j=HCH)
        onehot = sb("onehot", [128, NOH, 128], BF16)
        idx_stage = sb("idx_stage", [128, NB], I32)
        sorted_keys = keyA
        row_b = onehot[0:EP, :, :].rearrange("p a b -> p (a b)")[:, 0:EC]
        win_b = onehot[0:EP, :, :].rearrange("p a b -> p (a b)")[:, 1024:1024 + EC]
        spent_all = onehot[:, :, :].rearrange("p a b -> p (a b)").bitcast(F32)
        iota_i = row_of[:, 0:128].bitcast(I32)
        iota_f = sb("iota_f", [128, 128])
        iota_b = sb("iota_b", [128, 128], BF16)
        part_i = sb("part_i", [128, 1], I32)
        part_f = sb("part_f", [128, 1])
        sign_i = sb("sign_i", [128, 8], I32)
        sign_t = sb("sign_t", [128, 8], I32)
        sign = sb("sign", [128, 8])
        ident = sb("ident", [128, 128])
        ident_b = sb("ident_b", [128, 128], BF16)
        lower = sb("lower", [128, 128])
        heads = sb("heads", [128, 128])
        ones = sb("ones", [128, 256])
        zeros_b = sb("zeros_b", [128, 264], BF16)
        zeros = zeros_b[:, :].bitcast(F32)
        W_in = sb("W_in", [128, 2, C])
        WT = sb("WT", [128, 2, C])
        qkv = sb("qkv", [128, 2, 3 * C])
        WqT = sb("WqT", [128, 2, C])
        Wqc = sb("Wqc", [128, 2, C])
        proj = sb("proj", [128, 2, C])
        Wg1_in = sb("Wg1_in", [128, 2, GH])
        Wg1_g = sb("Wg1_g", [128, 2, GH])
        Wg2_b = sb("Wg2_b", [GH + 1, C])
        w1_sb = sb("w1_sb", [128, 2, HID])
        w2_sb = sb("w2_sb", [128, HC, C])
        lng = sb("lng", [128, 2])
        lnb = sb("lnb", [128, 2])
        lnb_wide = sb("lnb_wide", [128, 2, 128])
        b1_sb = sb("b1_sb", [128, HC])
        bias_row = sb("bias_row", [1, C])
        bg1_bc = sb("bg1_bc", [P, GH])
        bproj_bc = sb("bproj_bc", [P, C])
        b2_bc = sb("b2_bc", [P, C])
        wr_bc = sb("wr_bc", [P, C])
        br_bc = sb("br_bc", [P, 1])
        bn = sb("bn", [P, 2, 6])
        mv = sb("mv", [P, NW, 2])
        rstd = sb("rstd", [P, NW])
        nmr = sb("nmr", [P, NW])
        r2 = sb("r2", [P, NW])
        deg = sb("deg", [P, NW])
        norm = sb("norm", [P, NW])
        nwt = sb("nwt", [P, 3, NW])
        cnt = spent_all[:, 0 * NW:1 * NW]
        til = spent_all[:, 1 * NW:2 * NW]
        til_i = spent_all[:, 2 * NW:3 * NW].bitcast(I32)
        pad = spent_all[:, 3 * NW:4 * NW]
        pad_i = spent_all[:, 4 * NW:5 * NW].bitcast(I32)
        fill = spent_all[:, 6 * NW:7 * NW]
        scan = spent_all[:, 5 * NW:6 * NW]
        group_end = sb("group_end", [1, NW + 2], I32)
        xn = sb("xn", [P, 2, C])
        xT = sb("xT", [128, 2, 2, P])
        h_s = sb("h_s", [P, 2, C])
        h_res = sb("h_res", [P, 2, C])
        parts = sb("parts", [P, 2, 3, C], BF16)
        hg = sb("hg", [P, 2, GH])
        hgb = sb("hgb", [P, 2, GH])
        hact = sb("hact", [P, 2, GH])
        hgT = sb("hgT", [GH + 1, 2, P])
        kmax = sb("kmax", [128, 2])
        kmax2 = sb("kmax2", [128, 2])
        nkmax = sb("nkmax", [1, C])
        ek = xn
        vv_all = sb("vv", [128, 2, 2, 129])
        vv = vv_all[0:P, :, :, :]
        rden = sb("rden", [128, 2])
        ctxn = lnb_wide
        xt = h_s
        hself = parts[:, :, :, :].rearrange("p j a c -> p j (a c)")
        og = h_res
        ogT = W_in[:, 1, 0:2 * P].rearrange("p (c n) -> p c n", c=2)
        xb = W_in[0:P, 0, :]
        xm = keyA[0:P, 0 * C:1 * C]
        wz1 = sb("wz1", [P, 1])
        x1 = keyA[0:P, 1 * C:2 * C]
        z = keyA[0:P, 2 * C:3 * C]
        zw = keyA[0:P, 3 * C:4 * C]
        zT = vv_all[:, :, :, :].rearrange("p a b n -> p (a b n)")[:, 0:2 * P].rearrange("p (c n) -> p c n", c=2)
        hid = keyB[:, 0:HC * P].rearrange("p (k n) -> p k n", k=HC)
        mv2 = sb("mv2", [P, 2])
        rs2 = sb("rs2", [P, 3])
        wz = sb("wz", [P, NW])
        spent = spent_all[0:P, :]
        sel_i = spent[:, 0:NW].bitcast(I32)
        sel_m = spent[:, NW:2 * NW].bitcast(I32)
        half_k = spent[:, 2 * NW:4 * NW].rearrange("p (a w) -> p a w", a=2)
        mask = spent[:, 4 * NW:7 * NW].rearrange("p (a w) -> p a w", a=3)
        scr = spent[:, 7 * NW:8 * NW]
        csum = sb("csum", [P, 1])
        eqsum = sb("eqsum", [P, 1])
        thr = sb("thr", [P, 2])
        want = sb("want", [P, 2])
        tmp1 = sb("tmp1", [P, 2])
        coef = spent[:, 8 * NW:9 * NW]

        names = ("edges wload xload const const2 wprep wtp wev hotr hist stats nwt bn bna bg1 kps cntp chain sortd keyp "
                 "tabs tabfree final issued outs xn tp xT main hgv hgb erf hact gtp ghT gps gate hev split hout xstore "
                 "kT kmaxd kmt kmr stage kv ekv ctxp ctxd ctxn wqcp wqcd idx oh arrived used selfused staged "
                 "op og otp ogT pp xb xm sum x1 st nt zed zwt ztp zT hp gelu yp yv base csum").split()
        s = {n: sem("s_" + n) for n in names}
        s_slot = [sem(f"s_slot{j}") for j in range(NB)]
        s_hself = [sem(f"s_hself{j}") for j in range(2)]
        s_xt = [sem(f"s_xt{j}") for j in range(2)]
        s_tab = [sem(f"s_tab{j}") for j in range(2)]
        block = ctx.enter_context(nc.Block())

        src_v = src.rearrange("(p j) -> p j", p=EP)
        dst_v = dst.rearrange("(p j) -> p j", p=EP)
        x_v = x.rearrange("(p w) c -> p w c", w=NW)
        out_v = out.rearrange("(p w) c -> p w c", w=NW)
        tab_v = table.rearrange("(p w) c -> p w c", w=NW)
        OUTW = 5

        @block.sync
        def _(sp):
            sp.dma_start(e_int, src_v).then_inc(s["edges"], 16)
            sp.dma_start(col_of[0:EP, 0:EC], dst_v).then_inc(s["edges"], 16)
            sp.dma_start(big_g[:, 0:25, :], x_v[:, 0:25, :]).then_inc(s["xload"], 16)
            sp.dma_start(big_g[:, 25:50, :], x_v[:, 25:50, :]).then_inc(s["xload"], 16)
            loads = [
                (W_in[:, :, :], W.rearrange("(o p) i -> p o i", p=128)),
                (qkv[:, :, :], Wqkv.rearrange("(c p) n -> p c n", p=128)),
                (proj[:, :, :], Wproj.rearrange("(c p) n -> p c n", p=128)),
                (Wg1_in[:, :, :], Wg1.rearrange("(c p) n -> p c n", p=128)),
                (Wg2_b[0:GH, :], Wg2),
                (Wg2_b[GH:GH + 1, :], bg2.rearrange("(a n) -> a n", a=1)),
                (w1_sb[:, :, :], w1.rearrange("(c p) n -> p c n", p=128)),
                (w2_sb[:, :, :], w2.rearrange("(c p) n -> p c n", p=128)),
                (bias_row[:, :], bias.rearrange("(a n) -> a n", a=1)),
                (bg1_bc[:, :], bg1.rearrange("(a n) -> a n", a=1).to_broadcast([P, GH])),
                (bproj_bc[:, :], bproj.rearrange("(a n) -> a n", a=1).to_broadcast([P, C])),
                (b2_bc[:, :], b2.rearrange("(a n) -> a n", a=1).to_broadcast([P, C])),
                (wr_bc[:, :], wr.rearrange("n a -> a n").to_broadcast([P, C])),
                (br_bc[:, :], br.rearrange("(a n) -> a n", a=1).to_broadcast([P, 1])),
            ]
            for to, of in loads:
                sp.dma_start(to, of).then_inc(s["wload"], 16)
            with nc.allow_non_contiguous_dma(reason="three short vectors onto partitions"):
                sp.dma_start(lng[:, :], ln_g.rearrange("(c p) -> p c", p=128)).then_inc(s["wload"], 16)
                sp.dma_start(lnb[:, :], ln_b.rearrange("(c p) -> p c", p=128)).then_inc(s["wload"], 16)
                sp.dma_start(b1_sb[:, :], b1.rearrange("(c p) -> p c", p=128)).then_inc(s["wload"], 16)
            sp.sem_inc(s["tabfree"], 2)
            with sp.Fori(0, NPAIR) as i:
                for j in range(2):
                    sp.wait_ge(s["split"], i * 2 + (j + 3))
                    sp.dma_start(tab_v[:, bass.ds(i * 2 + j, 1), :].rearrange("p a c -> p (a c)"),
                                 parts[:, j, :, :].rearrange("p a c -> p (a c)")).then_inc(s_tab[j], 16)
                for j in range(2):
                    sp.wait_ge(s_tab[j], i * 16 + 16)
                    sp.sem_inc(s["tabfree"], 1)
            sp.wait_ge(s["tabs"], 2)
            rounds = sp.value_load(group_end[0:1, NW + 1:NW + 2], min_val=1, max_val=MAXG // ROUND)
            with sp.Fori(0, rounds) as i:
                for k in range(ROUND):
                    for j in range(k * GROUP, (k + 1) * GROUP):
                        sp.wait_ge(s_slot[j], i * 16 + 16)
                    sp.sem_inc(s["arrived"], 1)
            for g in range(NW // OUTW):
                sp.wait_ge(s["final"], (g + 1) * OUTW)
                sp.dma_start(out_v[:, g * OUTW:(g + 1) * OUTW, :],
                             big_g[:, g * OUTW:(g + 1) * OUTW, :]).then_inc(s["outs"], 16)
            sp.wait_ge(s["outs"], 16 * (NW // OUTW))

        @block.gpsimd
        def _(g):
            g.iota(iota_i[:, :], pattern=[[1, 128]], base=0, channel_multiplier=0).then_inc(s["const"], 1)
            g.iota(part_i[:, :], pattern=[[0, 1]], base=0, channel_multiplier=1).then_inc(s["const"], 1)
            g.memset(ident[:, :], 0.0).then_inc(s["const"], 1)
            g.memset(ones[:, :], 1.0).then_inc(s["const"], 1)
            g.memset(zeros[:, :], 0.0).then_inc(s["const"], 1)
            g.memset(vv_all[:, :, :, 128:129], 1.0).then_inc(s["const"], 1)
            g.wait_ge(s["const"], 6)
            g.affine_select(out=ident[:, :], in_=ident[:, :], compare_op=ALU.not_equal, fill=1.0, base=0,
                            pattern=[[-1, 128]], channel_multiplier=1).then_inc(s["const2"], 1)
            g.affine_select(out=lower[:, :], in_=ones[:, 0:128], compare_op=ALU.is_gt, fill=0.0, base=0,
                            pattern=[[1, 128]], channel_multiplier=-1).then_inc(s["const2"], 1)
            g.affine_select(out=heads[:, :], in_=ones[:, 0:128], compare_op=ALU.is_ge, fill=0.0, base=0,
                            pattern=[[-32, 4], [0, 32]], channel_multiplier=1).then_inc(s["const2"], 1)
            g.wait_ge(s["const2"], 3)
            g.affine_select(out=heads[:, :], in_=heads[:, :], compare_op=ALU.is_ge, fill=0.0, base=31,
                            pattern=[[32, 4], [0, 32]], channel_multiplier=-1).then_inc(s["const2"], 1)
            g.tensor_copy(ident_b[:, :], ident[:, :]).then_inc(s["const2"], 1)
            g.sem_inc(s["xstore"], 2)
            g.sem_inc(s["split"], 2)
            g.wait_ge(s["bg1"], 1)
            with g.Fori(0, NPAIR) as i:
                for j in range(2):
                    n = i * 2 + j + 1
                    g.wait_ge(s["hgv"], n)
                    g.sem_inc(s["issued"], 1)
                    g.tensor_tensor(hgb[:, j, :], hg[:, j, :], bg1_bc[:, :], ALU.add).then_inc(s["hgb"], 1)
                for j in range(2):
                    n = i * 2 + j + 1
                    g.wait_ge(s["xT"], n + 2)
                    g.sem_inc(s["issued"], 1)
                    g.tensor_copy(xnT[:, bass.ds(i * 2 + j, 1), :, :].rearrange("p a c n -> p (a c) n"),
                                  xT[:, j, :, :]).then_inc(s["xstore"], 1)
                    g.wait_ge(s["tabfree"], n)
                    g.sem_inc(s["issued"], 1)
                    g.wait_ge(s["hev"], n + 2)
                    g.sem_inc(s["issued"], 1)
                    g.tensor_copy(parts[:, j, 0, :], h_s[:, j, :]).then_inc(s["hout"], 1)
                    g.wait_ge(s["hout"], (i * 2 + j) * 3 + 1)
                    g.sem_inc(s["issued"], 1)
                    g.tensor_tensor(h_res[:, j, :], h_s[:, j, :], parts[:, j, 0, :], ALU.subtract).then_inc(s["hout"], 1)
                    g.wait_ge(s["hout"], (i * 2 + j) * 3 + 2)
                    g.sem_inc(s["issued"], 1)
                    g.tensor_copy(parts[:, j, 1, :], h_res[:, j, :]).then_inc(s["hout"], 1)
                    g.wait_ge(s["hout"], (i * 2 + j) * 3 + 3)
                    g.sem_inc(s["issued"], 1)
                    g.tensor_tensor(parts[:, j, 2, :], h_res[:, j, :], parts[:, j, 1, :], ALU.subtract).then_inc(s["split"], 1)
            g.wait_ge(s["xstore"], NW + 2)
            g.wait_ge(s["kT"], NW)
            with g.Fori(0, NPAIR) as i:
                for j in range(2):
                    g.wait_ge(s["kv"], i * 2 + j + 1)
                    g.sem_inc(s["issued"], 1)
                    g.tensor_copy(xT[:, j, :, :],
                                  xnT[:, bass.ds(i * 2 + j, 1), :, :].rearrange("p a c n -> p (a c) n")).then_inc(s["stage"], 1)
            for j in range(2):
                g.wait_ge(s_tab[j], 16 * NPAIR)
            g.wait_ge(s["tabs"], 2)
            last_row = g.to_reg(NODES - 1)
            rounds = g.value_load(group_end[0:1, NW + 1:NW + 2], min_val=1, max_val=MAXG // ROUND)
            with g.Fori(0, rounds) as i:
                for lo in (0, NB // 2):
                    g.wait_ge(s["used"], i * ROUND + (lo + NB // 2) // GROUP)
                    g.sem_inc(s["issued"], 1)
                    g.tensor_copy(idx_stage[:, lo:lo + NB // 2],
                                  col_of[:, bass.ds(i * NB + lo, NB // 2)]).then_inc(s["idx"], 1)
                    g.wait_ge(s["idx"], i * 2 + (1 if lo == 0 else 2))
                    g.sem_inc(s["issued"], 1)
                    for j in range(lo, lo + NB // 2):
                        g.indirect_dma_start(
                            out=gath[:, j, :], out_offset=None, in_=table[:, :],
                            in_offset=bass.IndirectOffsetOnAxis(ap=idx_stage[:, j:j + 1], axis=0),
                            bounds_check=last_row, oob_is_err=True).then_inc(s_slot[j], 16)

        @block.scalar
        def _(a):
            for n, free in (("xT", 2), ("hev", 2), ("gate", 2), ("ekv", 4), ("ogT", 1), ("zT", 1), ("gelu", 1)):
                a.sem_inc(s[n], free)
            a.wait_ge(s["wload"], 16 * 17)
            for c in range(2):
                a.activation(Wg1_g[:, c, :], Wg1_in[:, c, :], ACT.Identity, scale=lng[:, c:c + 1]).then_inc(s["wev"], 1)
            a.wait_ge(s["wtp"], 1)
            a.activation(WT[:, :, :], bank[0][:, :].rearrange("p (c n) -> p c n", c=2), ACT.Copy).then_inc(s["wev"], 1)
            a.activation(WqT[:, :, :], bank[1][:, :].rearrange("p (c n) -> p c n", c=2), ACT.Copy).then_inc(s["wev"], 1)
            a.wait_ge(s["stats"], 1)
            with a.Fori(0, NPAIR) as i:
                for j in range(2):
                    w = i * 2 + j
                    a.wait_ge(s["tp"], w + 1)
                    a.sem_inc(s["issued"], 1)
                    a.activation(xn[:, j, :], big_g[:, bass.ds(w, 1), :].rearrange("p a c -> p (a c)"), ACT.Identity,
                                 bias=nmr[:, bass.ds(w, 1)], scale=rstd[:, bass.ds(w, 1)]).then_inc(s["xn"], 1)
                for j in range(2):
                    w = i * 2 + j
                    a.wait_ge(s["tp"], w + 3)
                    a.wait_ge(s["main"], w + 1)
                    a.wait_ge(s["xstore"], w + 1)
                    a.activation(xT[:, j, :, :], bank[j][:, 0:2 * P].rearrange("p (c n) -> p c n", c=2),
                                 ACT.Copy).then_inc(s["xT"], 1)
                for j in range(2):
                    w = i * 2 + j
                    a.wait_ge(s["main"], w + 3)
                    a.sem_inc(s["issued"], 1)
                    a.activation(hg[:, j, :], bank[2 + j][0:P, 256:256 + GH], ACT.Identity,
                                 scale=r2[:, bass.ds(w, 1)]).then_inc(s["hgv"], 1)
                    a.wait_ge(s["split"], w + 1)
                    a.sem_inc(s["issued"], 1)
                    a.activation(h_s[:, j, :], bank[2 + j][0:P, 0:C], ACT.Identity,
                                 scale=norm[:, bass.ds(w, 1)]).then_inc(s["hev"], 1)
                for j in range(2):
                    w = i * 2 + j
                    a.wait_ge(s["hgb"], w + 1)
                    a.activation(hact[:, j, :], hgb[:, j, :], ACT.Gelu).then_inc(s["hact"], 1)
                for j in range(2):
                    w = i * 2 + j
                    a.wait_ge(s["gtp"], w + 1)
                    a.activation(hgT[0:GH, j, :], bank[5][0:GH, j * 128:j * 128 + P], ACT.Copy).then_inc(s["ghT"], 1)
                for j in range(2):
                    w = i * 2 + j
                    a.wait_ge(s["gps"], w + 1)
                    a.sem_inc(s["issued"], 1)
                    a.activation(big_g[:, bass.ds(w, 1), :].rearrange("p a c -> p (a c)"),
                                 bank[6 + j][0:P, 0:C], ACT.Tanh, scale=0.5).then_inc(s["gate"], 1)
            a.wait_ge(s["kmt"], 1)
            a.activation(nkmax[:, :], bank[0][0:1, 0:C], ACT.Copy, scale=-1.0).then_inc(s["kmr"], 1)
            with a.Fori(0, NPAIR) as i:
                for j in range(2):
                    w = i * 2 + j
                    a.wait_ge(s["kv"], w + 3)
                    a.wait_ge(s["ctxp"], w + 1)
                    a.activation(ek[:, j, :], bank[2 + j][0:P, 0:C], ACT.Exp).then_inc(s["ekv"], 1)
                    a.activation(vv[:, j, :, 0:128], bank[2 + j][0:P, C:2 * C].rearrange("p (h n) -> p h n", h=2),
                                 ACT.Copy).then_inc(s["ekv"], 1)
            a.wait_ge(s["wqcd"], 1)
            for j in range(2):
                a.wait_ge(s_tab[j], 16 * NPAIR)

            def loads(m, j):
                a.wait_ge(s["selfused"], m + 1)
                a.dma_start(hself[:, j, :], tab_v[:, bass.ds(m, 1), :].rearrange("p a c -> p (a c)")).then_inc(s_hself[j], 16)
                a.wait_ge(s["xm"], m + 1)
                a.dma_start(xt[:, j, :], x_v[:, bass.ds(m, 1), :].rearrange("p a c -> p (a c)")).then_inc(s_xt[j], 16)

            def stage(m):
                a.wait_ge(s["op"], m + 1)
                a.sem_inc(s["issued"], 1)
                a.activation(xT[:, 0, :, :], xnT[:, bass.ds(m, 1), :, :].rearrange("p a c n -> p (a c) n"),
                             ACT.Copy).then_inc(s["staged"], 1)

            def gated(m):
                a.wait_ge(s["otp"], m + 2)
                a.activation(ogT[:, :, :], bank[2][:, 0:2 * P].rearrange("p (c n) -> p c n", c=2),
                             ACT.Copy).then_inc(s["ogT"], 1)

            def hidden(m):
                a.wait_ge(s["ztp"], m + 2)
                a.activation(zT[:, :, :], bank[4][:, 0:2 * P].rearrange("p (c n) -> p c n", c=2),
                             ACT.Copy).then_inc(s["zT"], 1)
                for k in range(HC):
                    if k % 4 == 0:
                        a.wait_ge(s["hp"], m * 2 + (k // 4 + 1))
                        a.wait_ge(s["yp"], m + 1)
                    a.activation(hid[:, k, :], bank[5 + k // 4][:, (k % 4) * P:(k % 4 + 1) * P], ACT.Gelu_apprx_tanh,
                                 bias=b1_sb[:, k:k + 1]).then_inc(s["gelu"], 1)

            def window(w, j, first=False, last=False):
                if not last:
                    loads(w + 1, 1 - j)
                    stage(w + 1)
                if not first:
                    hidden(w - 1)
                if not last:
                    gated(w + 1)

            loads(0, 0)
            stage(0)
            gated(0)
            window(0, 0, first=True)
            with a.Fori(0, NPAIR - 1) as i:
                window(i * 2 + 1, 1)
                window(i * 2 + 2, 0)
            window(NW - 1, 1, last=True)
            hidden(NW - 1)

        @block.tensor
        def _(t):
            for n, free in (("tp", 2), ("main", 2), ("kv", 2), ("ctxp", 2), ("selfused", 2), ("used", ROUND), ("op", 1),
                            ("otp", 1), ("ztp", 1), ("yp", 1)):
                t.sem_inc(s[n], free)
            t.wait_ge(s["wload"], 16 * 17)
            t.wait_ge(s["const2"], 5)
            for c in range(2):
                for o in range(2):
                    t.transpose(bank[0][:, c * C + o * 128:c * C + (o + 1) * 128],
                                W_in[:, o, c * 128:(c + 1) * 128], ident[:, :])
            for c in range(2):
                for o in range(2):
                    last = t.transpose(bank[1][:, c * C + o * 128:c * C + (o + 1) * 128],
                                       qkv[:, o, c * 128:(c + 1) * 128], ident[:, :])
            last.then_inc(s["wtp"], 1)
            t.matmul(bank[3][0:P, 0:NW], ident_b[:, 0:P], zeros_b[:, 0:NW], start=True, stop=False, skip_group_check=True)
            for n in range(NHIST):
                t.wait_ge(s["hotr"], n + 1)
                with t.Fori(0, HCH // 8) as i:
                    for u in range(8):
                        t.matmul(bank[3][0:P, 0:NW], hot_row[:, :, bass.ds(i * 8 + u, 1)].rearrange("p r a -> p (r a)"),
                                 hot_win[:, :, bass.ds(i * 8 + u, 1)].rearrange("p w a -> p (w a)"),
                                 start=False, stop=False, skip_group_check=True)
                t.matmul(bank[3][0:P, 0:NW], ident_b[:, 0:P], zeros_b[:, 0:NW], start=False, stop=n == NHIST - 1,
                         skip_group_check=True).then_inc(s["hist"], 1)
            t.wait_ge(s["wprep"], 1)
            for c in range(2):
                last = t.matmul(bank[2][0:P, 0:GH], lnb_wide[:, c, 0:P], Wg1_in[:, c, :], start=c == 0, stop=c == 1)
            last.then_inc(s["kps"], 1)
            t.wait_ge(s["nwt"], 1)
            t.matmul(bank[4][:, 0:NW], ones[0:P, 0:128], deg[:, :], start=True, stop=True).then_inc(s["cntp"], 1)
            t.wait_ge(s["wev"], 4)
            t.wait_ge(s["bg1"], 1)
            with t.Fori(0, NPAIR) as i:
                for j in range(2):
                    w = i * 2 + j
                    t.wait_ge(s["xn"], w + 1)
                    t.wait_ge(s["xT"], w + 1)
                    for c in range(2):
                        last = t.transpose(bank[j][:, c * P:(c + 1) * P], xn[:, j, c * 128:(c + 1) * 128], ident[0:P, 0:P])
                    last.then_inc(s["tp"], 1)
                for j in range(2):
                    w = i * 2 + j
                    t.wait_ge(s["xT"], w + 3)
                    t.wait_ge(s["hev"], w + 1)
                    for c in range(2):
                        t.matmul(bank[2 + j][0:P, C:C + GH], xT[:, j, c, :], Wg1_g[:, c, :], start=c == 0, stop=c == 1)
                    for c in range(2):
                        t.matmul(bank[2 + j][0:P, 0:C], xT[:, j, c, :], WT[:, c, :], start=c == 0, stop=False)
                    t.matmul(bank[2 + j][0:P, 0:C], ones[0:1, 0:P], bias_row[:, :], start=False, stop=True).then_inc(s["main"], 1)
                    if j == 0:
                        t.wait_ge(s["kmaxd"], i + 1)
                    for half in range(2):
                        for c in range(2):
                            last = t.matmul(bank[4][:, half * 256 + j * P:half * 256 + (j + 1) * P],
                                            qkv[:, c, C + half * 128:C + (half + 1) * 128], xT[:, j, c, :],
                                            start=c == 0, stop=c == 1)
                    last.then_inc(s["kT"], 1)
                for j in range(2):
                    w = i * 2 + j
                    t.wait_ge(s["hact"], w + 1)
                    t.sem_inc(s["issued"], 1)
                    t.transpose(bank[5][0:GH, j * 128:j * 128 + P], hact[:, j, :], ident[0:P, 0:P]).then_inc(s["gtp"], 1)
                    if j == 0:
                        t.wait_ge(s["ghT"], w + 1)
                for j in range(2):
                    w = i * 2 + j
                    t.wait_ge(s["ghT"], w + 1)
                    t.wait_ge(s["gate"], w + 1)
                    t.matmul(bank[6 + j][0:P, 0:C], hgT[:, j, :], Wg2_b[:, :], start=True, stop=True).then_inc(s["gps"], 1)
            t.wait_ge(s["kmaxd"], NPAIR + 1)
            t.wait_ge(s["gate"], NW + 2)
            for half in range(2):
                last = t.transpose(bank[0][0:1, half * 128:(half + 1) * 128], kmax[:, half:half + 1], ident[:, :])
            last.then_inc(s["kmt"], 1)
            for half in range(2):
                t.matmul(bank[6 + half][:, 0:129], ident[:, :], zeros[:, 0:129], start=True, stop=False, skip_group_check=True)
            t.wait_ge(s["kmr"], 1)
            with t.Fori(0, NPAIR) as i:
                for j in range(2):
                    w = i * 2 + j
                    t.wait_ge(s["stage"], w + 1)
                    t.wait_ge(s["ekv"], w * 2 + 2)
                    for c in range(2):
                        t.matmul(bank[2 + j][0:P, 0:C], xT[:, j, c, :], qkv[:, c, C:2 * C], start=c == 0, stop=False)
                    t.matmul(bank[2 + j][0:P, 0:C], ones[0:1, 0:P], nkmax[:, :], start=False, stop=True)
                    for c in range(2):
                        last = t.matmul(bank[2 + j][0:P, C:2 * C], xT[:, j, c, :], qkv[:, c, 2 * C:3 * C], start=c == 0, stop=c == 1)
                    last.then_inc(s["kv"], 1)
                for j in range(2):
                    w = i * 2 + j
                    t.wait_ge(s["ekv"], w * 2 + 6)
                    for half in range(2):
                        last = t.matmul(bank[6 + half][:, 0:129], ek[:, j, half * 128:(half + 1) * 128], vv[:, j, half, :],
                                        start=False, stop=False, skip_group_check=True)
                    last.then_inc(s["ctxp"], 1)
            for half in range(2):
                last = t.matmul(bank[6 + half][:, 0:129], ident[:, :], zeros[:, 0:129], start=False, stop=True, skip_group_check=True)
            last.then_inc(s["ctxd"], 1)
            t.wait_ge(s["sortd"], 1)
            for b in range(COLS // 128):
                last = t.transpose(bank[b // 4][:, (b % 4) * 128:(b % 4 + 1) * 128], sorted_keys[:, b * 128:(b + 1) * 128], ident[:, :])
            last.then_inc(s["keyp"], 1)
            t.wait_ge(s["ctxn"], 1)
            for c in range(2):
                for half in range(2):
                    last = t.matmul(bank[4][:, c * C + half * 128:c * C + (half + 1) * 128],
                                    WqT[:, half, c * 128:(c + 1) * 128], ctxn[:, half, :], start=True, stop=True)
            last.then_inc(s["wqcp"], 1)
            t.wait_ge(s["wqcd"], 1)
            t.wait_ge(s["tabs"], 2)

            def sums(w, j, nth):
                t.wait_ge(s_hself[j], nth * 16 + 16)
                t.wait_ge(s["x1"], w + 1)
                for k in range(3):
                    last = t.matmul(bank[0][0:P, 0:C], ident_b[0:P, 0:P], hself[:, j, k * C:(k + 1) * C],
                                    start=k == 0, stop=False, skip_group_check=True)
                last.then_inc(s["selfused"], 1)
                first = t.value_load(group_end[0:1, bass.ds(w, 1)], min_val=0, max_val=MAXG - 1)
                end = t.value_load(group_end[0:1, bass.ds(w + 1, 1)], min_val=1, max_val=MAXG)
                with t.Fori(first, end) as q:
                    t.wait_ge(s["oh"], q + 1)
                    t.wait_ge(s["arrived"], q + 1)
                    for u in range(GROUP):
                        for k in range(3):
                            last = t.matmul(bank[0][0:P, 0:C],
                                            onehot[:, bass.ds((q % ROUND) * GROUP + u, 1), 0:P].rearrange("p a r -> p (a r)"),
                                            gath[:, bass.ds((q % ROUND) * GROUP + u, 1), k * C:(k + 1) * C]
                                            .rearrange("p a c -> p (a c)"),
                                            start=False, stop=False, skip_group_check=True)
                    last.then_inc(s["used"], 1)
                t.matmul(bank[0][0:P, 0:C], ident_b[:, 0:P], zeros_b[:, 0:C], start=False, stop=True,
                         skip_group_check=True).then_inc(s["sum"], 1)

            def attention(m):
                t.wait_ge(s["staged"], m + 1)
                t.wait_ge(s["og"], m + 1)
                for c in range(2):
                    last = t.matmul(bank[1][0:P, 0:C], xT[:, 0, c, :], Wqc[:, c, :], start=c == 0, stop=c == 1)
                last.then_inc(s["op"], 1)

            def turn_gated(m):
                t.wait_ge(s["og"], m + 2)
                t.wait_ge(s["ogT"], m + 1)
                for c in range(2):
                    last = t.transpose(bank[2][:, c * P:(c + 1) * P], og[:, 0, c * 128:(c + 1) * 128], ident[0:P, 0:P])
                last.then_inc(s["otp"], 1)

            def project(m):
                t.wait_ge(s["ogT"], m + 2)
                t.wait_ge(s["xm"], m + 2)
                for c in range(2):
                    last = t.matmul(bank[3][0:P, 0:C], ogT[:, c, :], proj[:, c, :], start=c == 0, stop=c == 1)
                last.then_inc(s["pp"], 1)

            def turn_z(m):
                t.wait_ge(s["zed"], m + 1)
                t.wait_ge(s["zT"], m + 1)
                for c in range(2):
                    last = t.transpose(bank[4][:, c * P:(c + 1) * P], z[:, c * 128:(c + 1) * 128], ident[0:P, 0:P])
                last.then_inc(s["ztp"], 1)

            def up(m):
                t.wait_ge(s["zT"], m + 2)
                t.wait_ge(s["gelu"], m * HC + 1)
                for k in range(HC):
                    for c in range(2):
                        last = t.matmul(bank[5 + k // 4][:, (k % 4) * P:(k % 4 + 1) * P],
                                        w1_sb[:, c, k * 128:(k + 1) * 128], zT[:, c, :], start=c == 0, stop=c == 1)
                    if k % 4 == 3:
                        last.then_inc(s["hp"], 1)

            def down(m):
                t.wait_ge(s["yv"], m + 1)
                for k in range(HC):
                    if k % 4 == 0:
                        t.wait_ge(s["gelu"], m * HC + (k + 5))
                    last = t.matmul(bank[7][0:P, 0:C], hid[:, k, :], w2_sb[:, k, :], start=k == 0, stop=k == HC - 1)
                last.then_inc(s["yp"], 1)

            def window(w, j, nth, first=False, last=False):
                sums(w, j, nth)
                if not first:
                    turn_z(w - 1)
                if not last:
                    attention(w + 1)
                if not first:
                    up(w - 1)
                if not last:
                    turn_gated(w + 1)
                if not first:
                    down(w - 1)
                if not last:
                    project(w + 1)

            attention(0)
            turn_gated(0)
            project(0)
            window(0, 0, 0, first=True)
            with t.Fori(0, NPAIR - 1) as i:
                window(i * 2 + 1, 1, i)
                window(i * 2 + 2, 0, i + 1)
            window(NW - 1, 1, NPAIR - 1, last=True)
            turn_z(NW - 1)
            up(NW - 1)
            down(NW - 1)
            for n in range(32):
                t.wait_ge(s["csum"], n + 1)
                t.matmul(bank[0][0:P, 0:1], ones[0:P, 0:P], csum[:, :], start=True, stop=True).then_inc(s["cntp"], 1)
            t.wait_ge(s["csum"], 33)
            t.matmul(bank[0][0:P, 0:1], ones[0:P, 0:P], csum[:, :], start=True, stop=True)
            t.matmul(bank[1][0:P, 0:1], lower[0:P, 0:P], eqsum[:, :], start=True, stop=True).then_inc(s["cntp"], 1)

        @block.vector
        def _(v):
            made = [0]

            def step(ins):
                made[0] += 1
                ins.then_inc(s["chain"], 1)
                v.wait_ge(s["chain"], made[0])

            v.wait_ge(s["const"], 6)
            step(nc.vector.memset(hgT[GH:GH + 1, :, :], 1.0))
            step(nc.vector.tensor_copy(iota_f[:, :], iota_i[:, :]))
            step(nc.vector.tensor_copy(iota_b[:, :], iota_f[:, :]))
            step(nc.vector.tensor_copy(part_f[:, :], part_i[:, :]))
            for m in range(8):
                step(nc.vector.tensor_scalar(sign_i[:, m:m + 1], part_i[:, :], max(m - 1, 0), None, ALU.logical_shift_right))
            for m in range(8):
                if m == 0:
                    step(nc.vector.tensor_copy(sign_t[:, m:m + 1], sign_i[:, m:m + 1]))
                else:
                    step(nc.vector.tensor_scalar(sign_t[:, m:m + 1], sign_i[:, m:m + 1], 1, None, ALU.logical_shift_right))
                    step(nc.vector.tensor_tensor(sign_t[:, m:m + 1], sign_t[:, m:m + 1], sign_i[:, m:m + 1], ALU.bitwise_xor))
            step(nc.vector.tensor_scalar(sign_t[:, :], sign_t[:, :], 1, None, ALU.bitwise_and))
            step(nc.vector.tensor_copy(sign[:, :], sign_t[:, :]))
            step(nc.vector.tensor_scalar(sign[:, :], sign[:, :], -2.0, 1.0, ALU.mult, ALU.add))
            v.wait_ge(s["edges"], 32)
            step(nc.vector.tensor_copy(keyA[0:EP, 0:EC], e_int))
            row_i = row_of[0:EP, 0:EC].bitcast(I32)
            step(nc.vector.tensor_scalar(row_i, keyA[0:EP, 0:EC], 1.0 / NW, -0.49, ALU.mult, ALU.add))
            step(nc.vector.tensor_copy(row_b, row_i))
            step(nc.vector.scalar_tensor_tensor(keyA[0:EP, 0:EC], row_i, -float(NW), keyA[0:EP, 0:EC], ALU.mult, ALU.add))
            step(nc.vector.tensor_copy(win_b, keyA[0:EP, 0:EC]))
            step(nc.vector.tensor_copy(e_int, keyA[0:EP, 0:EC]))

            def histogram(n):
                if n:
                    v.wait_ge(s["hist"], n)
                at = slice(n * HCH, (n + 1) * HCH)
                for w in range(NW):
                    nc.vector.tensor_scalar(hot_win[:, w, :], win_b[:, at], float(w), None, ALU.is_equal)
                for r in range(P):
                    last = nc.vector.tensor_scalar(hot_row[:, r, :], row_b[:, at], float(r), None, ALU.is_equal)
                last.then_inc(s["hotr"], 1)

            def node_stats(w):
                nc.vector.bn_stats(bn[:, w % 2, :], big_g[:, w, :]).then_inc(s["bn"], 1)
                v.wait_ge(s["bn"], w + 1)
                nc.vector.bn_aggr(mv[:, w, :], bn[:, w % 2, :]).then_inc(s["bna"], 1)

            def inverse_sqrt(to, of, t):
                step(nc.vector.tensor_scalar(t.bitcast(I32), of.bitcast(I32), 1, None, ALU.logical_shift_right))
                step(nc.vector.tensor_scalar(to.bitcast(I32), t.bitcast(I32), -1.0, float(0x5F3759DF), ALU.mult, ALU.add))
                for _ in range(NEWTON):
                    step(nc.vector.tensor_tensor(t, to, to, ALU.mult))
                    step(nc.vector.tensor_tensor(t, t, of, ALU.mult))
                    step(nc.vector.tensor_scalar(t, t, -0.5, 1.5, ALU.mult, ALU.add))
                    step(nc.vector.tensor_tensor(to, to, t, ALU.mult))

            histogram(0)
            step(nc.vector.memset(keyA[:, :], EMPTY))
            step(nc.vector.tensor_scalar(e_int, e_int, COLBITS + ROWBITS, BASE, ALU.logical_shift_left, ALU.bitwise_or))
            step(nc.vector.tensor_scalar(row_i, row_i, COLBITS, None, ALU.logical_shift_left))
            step(nc.vector.tensor_tensor(e_int, e_int, row_i, ALU.bitwise_or))
            step(nc.vector.tensor_tensor(keyA[0:EP, 0:EC].bitcast(I32), e_int, col_of[0:EP, 0:EC], ALU.bitwise_or))
            v.wait_ge(s["wload"], 16 * 17)
            for c in range(2):
                last = nc.vector.tensor_scalar(lnb_wide[:, c, :], ones[:, 0:128], lnb[:, c:c + 1], None, ALU.mult)
            last.then_inc(s["wprep"], 1)
            v.wait_ge(s["xload"], 32)
            for w in range(NW // 2):
                node_stats(w)
            histogram(1)
            for w in range(NW // 2, NW):
                node_stats(w)
            v.wait_ge(s["bna"], NW)
            step(nc.vector.tensor_scalar(nwt[:, 0, :], mv[:, :, 1], EPS, None, ALU.add))
            inverse_sqrt(rstd[:, :], nwt[:, 0, :], nwt[:, 1, :])
            step(nc.vector.scalar_tensor_tensor(nmr[:, :], mv[:, :, 0], -1.0, rstd[:, :], ALU.mult, ALU.mult))
            step(nc.vector.tensor_tensor(nwt[:, 0, :], mv[:, :, 1], rstd[:, :], ALU.mult))
            step(nc.vector.tensor_tensor(nwt[:, 0, :], nwt[:, 0, :], rstd[:, :], ALU.mult))
            step(nc.vector.tensor_scalar(nwt[:, 0, :], nwt[:, 0, :], EPS, None, ALU.add))
            inverse_sqrt(r2[:, :], nwt[:, 0, :], nwt[:, 1, :])
            histogram(2)
            histogram(3)
            v.wait_ge(s["hist"], NHIST)
            nc.vector.tensor_copy(deg[:, :], bank[3][0:P, 0:NW]).then_inc(s["nwt"], 1)
            v.wait_ge(s["nwt"], 1)
            step(nc.vector.tensor_scalar(nwt[:, 0, :], deg[:, :], 1.0, None, ALU.add))
            inverse_sqrt(norm[:, :], nwt[:, 0, :], nwt[:, 1, :])
            nc.vector.memset(kmax[:, :], -3.0e38).then_inc(s["stats"], 1)
            v.wait_ge(s["kps"], 1)
            nc.vector.tensor_tensor(bg1_bc[:, :], bank[2][0:P, 0:GH], bg1_bc[:, :], ALU.add).then_inc(s["bg1"], 1)
            v.wait_ge(s["cntp"], 1)
            nc.vector.tensor_copy(cnt[:, :], bank[4][:, 0:NW]).then_inc(s["kmaxd"], 1)
            v.wait_ge(s["kmaxd"], 1)
            step(nc.vector.tensor_scalar(til_i[:, :], cnt[:, :], 1.0 / GEDGE, 0.5 - 0.5 / GEDGE, ALU.mult, ALU.add))
            step(nc.vector.tensor_scalar(til[:, :], til_i[:, :], 1.0, None, ALU.max))
            step(nc.vector.scalar_tensor_tensor(pad[:, :], til[:, :], float(GEDGE), cnt[:, :], ALU.mult, ALU.subtract))
            step(nc.vector.tensor_scalar(cnt[:, :], iota_f[:, 0:NW], -float(NOWIN), None, ALU.add))
            for k in range(GROUP):
                step(nc.vector.tensor_scalar(fill[:, :], pad[:, :], -float(TILE * k), part_f[:, :], ALU.add, ALU.is_gt))
                step(nc.vector.tensor_tensor(fill[:, :], fill[:, :], cnt[:, :], ALU.mult))
                step(nc.vector.tensor_scalar(pad_i[:, :], fill[:, :], float(NOWIN), None, ALU.add))
                step(nc.vector.tensor_scalar(keyA[:, EC + k * NW:EC + (k + 1) * NW].bitcast(I32), pad_i[:, :],
                                             COLBITS + ROWBITS, BASE | NOROW << COLBITS,
                                             ALU.logical_shift_left, ALU.bitwise_or))
            step(nc.vector.tensor_tensor_scan(scan[:, :], ones[:, 0:NW], til[:, :], 0.0, ALU.mult, ALU.add))
            step(nc.vector.memset(group_end[:, 0:1], 0))
            step(nc.vector.tensor_copy(group_end[:, 1:NW], scan[0:1, 0:NW - 1]))
            step(nc.vector.tensor_scalar(group_end[:, NW + 1:NW + 2], scan[0:1, NW - 1:NW], 1.0 / ROUND,
                                         (ROUND - 1.0) / ROUND - 0.5 + 0.5 / ROUND, ALU.mult, ALU.add))
            step(nc.vector.tensor_scalar(group_end[:, NW:NW + 1], group_end[:, NW + 1:NW + 2], float(ROUND), None, ALU.mult))

            cur = [keyA, keyB]
            stages = [0]
            peeks = [0]

            def peek():
                n = peeks[0]
                if n < NPAIR and stages[0] % 5 == 0:
                    v.wait_ge(s["kT"], 2 * n + 2)
                    step(nc.vector.tensor_reduce(kmax2[:, :], bank[4][:, :].rearrange("p (h n) -> p h n", h=2)[:, :, 0:2 * P],
                                                 AX.X, ALU.max))
                    nc.vector.tensor_tensor(kmax[:, :], kmax[:, :], kmax2[:, :], ALU.max).then_inc(s["kmaxd"], 1)
                    peeks[0] += 1

            def exchange(lo_in, hi_in, lo_out, hi_out):
                nc.vector.tensor_tensor(lo_out, lo_in, hi_in, ALU.min).then_inc(s["chain"], 1)
                nc.vector.tensor_tensor(hi_out, lo_in, hi_in, ALU.max).then_inc(s["chain"], 1)
                made[0] += 2
                v.wait_ge(s["chain"], made[0])
                cur.reverse()
                stages[0] += 1
                peek()

            def distance(d):
                a, b = (k[:, :].rearrange("p (n two d) -> p n two d", two=2, d=d) for k in cur)
                exchange(a[:, :, 0, :], a[:, :, 1, :], b[:, :, 0, :], b[:, :, 1, :])

            def swap_blocks():
                step(nc.vector.transpose(cur[1][:, :], cur[0][:, :]))
                cur.reverse()

            def turn(m):
                step(nc.vector.tensor_scalar(cur[0][:, :], cur[0][:, :], sign[:, m:m + 1], None, ALU.mult))

            turn(0)
            for k in range(1, LOGF + 1):
                size = 1 << k
                a, b = (q[:, :].rearrange("p (n s) -> p n s", s=size) for q in cur)
                hi = a[:, :, size - 1:size // 2 - 1:-1] if size > 2 else a[:, :, 1:2]
                exchange(a[:, :, 0:size // 2], hi, b[:, :, 0:size // 2], b[:, :, size // 2:size])
                for e in range(k - 2, -1, -1):
                    distance(1 << e)
            for m in range(1, 8):
                turn(m)
                if m >= 7:
                    a, b = cur
                    step(nc.vector.tensor_tensor(b[0:64, :], a[0:64, :], a[64:128, :], ALU.min))
                    step(nc.vector.tensor_tensor(b[64:128, :], a[0:64, :], a[64:128, :], ALU.max))
                    cur.reverse()
                if m >= 6:
                    a, b = cur
                    for q in (0, 64):
                        step(nc.vector.tensor_tensor(b[q:q + 32, :], a[q:q + 32, :], a[q + 32:q + 64, :], ALU.min))
                        step(nc.vector.tensor_tensor(b[q + 32:q + 64, :], a[q:q + 32, :], a[q + 32:q + 64, :], ALU.max))
                    cur.reverse()
                swap_blocks()
                for e in range(min(m, 5) - 1, -1, -1):
                    distance(1 << e)
                swap_blocks()
                for e in range(LOGF - 1, 6 if m == 7 else -1, -1):
                    distance(1 << e)
            while peeks[0] < NPAIR:
                stages[0] = 0
                peek()
            v.wait_ge(s["kmaxd"], NPAIR + 1)
            assert cur[0] is sorted_keys
            v.sem_inc(s["sortd"], 1)
            v.wait_ge(s["keyp"], 1)
            spare = cur[1]
            for h in range(2):
                step(nc.vector.tensor_copy(spare[:, h * 512:(h + 1) * 512], bank[h][:, :]))
            keys_i = spare[:, :].bitcast(I32).rearrange("q (b p) -> q b p", b=8)
            nc.vector.tensor_scalar(col_of[:, :].rearrange("q (p b) -> q b p", b=8), keys_i, (1 << COLBITS) - 1, None,
                                    ALU.bitwise_and).then_inc(s["tabs"], 1)
            step(nc.vector.tensor_scalar(cur[0][:, :].bitcast(I32).rearrange("q (b p) -> q b p", b=8), keys_i, COLBITS,
                                         (1 << ROWBITS) - 1, ALU.logical_shift_right, ALU.bitwise_and))
            nc.vector.tensor_copy(row_of[:, :].rearrange("q (p b) -> q b p", b=8),
                                  cur[0][:, :].bitcast(I32).rearrange("q (b p) -> q b p", b=8)).then_inc(s["tabs"], 1)
            v.wait_ge(s["ctxd"], 1)
            for half in range(2):
                step(nc.vector.reciprocal(rden[:, half:half + 1], bank[6 + half][:, 128:129]))
            for half in range(2):
                last = nc.vector.scalar_tensor_tensor(ctxn[:, half, :], bank[6 + half][:, 0:128], rden[:, half:half + 1],
                                                      heads[:, :], ALU.mult, ALU.mult)
                if half == 0:
                    step(last)
            last.then_inc(s["ctxn"], 1)
            v.wait_ge(s["wqcp"], 1)
            nc.vector.tensor_scalar(Wqc[:, :, :], bank[4][:, :].rearrange("p (c n) -> p c n", c=2), 0.5, None,
                                    ALU.mult).then_inc(s["wqcd"], 1)
            v.wait_ge(s["tabs"], 2)
            for n in ("x1", "og", "yv"):
                v.sem_inc(s[n], 1)
            v.sem_inc(s["xm"], 2)

            def hots(m):
                first = v.value_load(group_end[0:1, bass.ds(m, 1)], min_val=0, max_val=MAXG - 1)
                end = v.value_load(group_end[0:1, bass.ds(m + 1, 1)], min_val=1, max_val=MAXG)
                with v.Fori(first, end) as q:
                    v.wait_ge(s["used"], q + 1)
                    for u in range(GROUP):
                        last = nc.vector.tensor_scalar(
                            onehot[:, bass.ds((q % ROUND) * GROUP + u, 1), 0:P].rearrange("p a r -> p (a r)"),
                            iota_b[:, 0:P], row_of[:, bass.ds(q * GROUP + u, 1)], None, ALU.is_equal)
                    last.then_inc(s["oh"], 1)

            def gate_of(m):
                return big_g[:, bass.ds(m, 1), :].rearrange("p a c -> p (a c)")

            def gated(m):
                v.wait_ge(s["op"], m + 2)
                v.wait_ge(s["otp"], m + 1)
                nc.vector.scalar_tensor_tensor(og[:, 0, :], gate_of(m), 1.0, bank[1][0:P, 0:C],
                                               ALU.add, ALU.mult).then_inc(s["og"], 1)

            def mixed(m, j, nth):
                v.wait_ge(s_xt[j], nth * 16 + 16)
                nc.vector.tensor_tensor(xb[:, :], xt[:, j, :], bproj_bc[:, :], ALU.add).then_inc(s["xb"], 1)
                v.wait_ge(s["xb"], m + 1)
                v.wait_ge(s["pp"], m + 1)
                nc.vector.tensor_tensor(xm[:, :], bank[3][0:P, 0:C], xb[:, :], ALU.add).then_inc(s["xm"], 1)

            def normed(w):
                wi = bass.ds(w, 1)
                v.wait_ge(s["xm"], w + 3)
                v.wait_ge(s["sum"], w + 1)
                nc.vector.scalar_tensor_tensor(x1[:, :], bank[0][0:P, 0:C], norm[:, wi], xm[:, :],
                                               ALU.mult, ALU.add).then_inc(s["x1"], 1)
                v.wait_ge(s["x1"], w + 2)
                nc.vector.bn_stats(bn[:, 0, :], x1[:, :]).then_inc(s["st"], 1)
                v.wait_ge(s["st"], w * 2 + 1)
                v.sem_inc(s["issued"], 1)
                nc.vector.bn_aggr(mv2[:, :], bn[:, 0, :]).then_inc(s["st"], 1)
                v.wait_ge(s["st"], w * 2 + 2)
                var, root, t0 = rs2[:, 0:1], rs2[:, 1:2], rs2[:, 2:3]
                ops = [lambda: nc.vector.tensor_scalar(var, mv2[:, 1:2], EPS, None, ALU.add),
                       lambda: nc.vector.tensor_scalar(t0.bitcast(I32), var.bitcast(I32), 1, None, ALU.logical_shift_right),
                       lambda: nc.vector.tensor_scalar(root.bitcast(I32), t0.bitcast(I32), -1.0, float(0x5F3759DF),
                                                       ALU.mult, ALU.add)]
                for _ in range(NEWTON):
                    ops += [lambda: nc.vector.tensor_scalar(t0, root, root, var, ALU.mult, ALU.mult),
                            lambda: nc.vector.tensor_scalar(t0, t0, -0.5, 1.5, ALU.mult, ALU.add),
                            lambda: nc.vector.tensor_tensor(root, root, t0, ALU.mult)]
                for n, op in enumerate(ops):
                    op().then_inc(s["nt"], 1)
                    v.wait_ge(s["nt"], w * len(ops) + (n + 1))
                v.wait_ge(s["ztp"], w + 1)
                nc.vector.tensor_scalar(z[:, :], x1[:, :], mv2[:, 0:1], root, ALU.subtract, ALU.mult).then_inc(s["zed"], 1)
                v.wait_ge(s["zed"], w + 1)
                nc.vector.tensor_tensor_reduce(out=zw[:, :], in0=z[:, :], in1=wr_bc[:, :], scale=1.0, scalar=0.0,
                                               op0=ALU.mult, op1=ALU.add, accum_out=wz1[:, :]).then_inc(s["zwt"], 1)
                nc.vector.tensor_tensor(gate_of(w), x1[:, :], z[:, :], ALU.add).then_inc(s["base"], 1)
                v.wait_ge(s["zwt"], w + 1)
                nc.vector.tensor_tensor(wz[:, wi], wz1[:, :], br_bc[:, :], ALU.add).then_inc(s["base"], 1)

            def fed(m):
                v.wait_ge(s["yp"], m + 2)
                nc.vector.tensor_tensor(y_all[:, bass.ds(m, 1), :].rearrange("p a c -> p (a c)"), bank[7][0:P, 0:C],
                                        b2_bc[:, :], ALU.add).then_inc(s["yv"], 1)

            def window(w, j, nth, first=False, last=False):
                if not last:
                    gated(w + 1)
                normed(w)
                if not last:
                    hots(w + 1)
                if not first:
                    fed(w - 1)
                if not last:
                    mixed(w + 1, 1 - j, nth)

            hots(0)
            gated(0)
            mixed(0, 0, 0)
            window(0, 0, 0, first=True)
            with v.Fori(0, NPAIR - 1) as i:
                window(i * 2 + 1, 1, i + 1)
                window(i * 2 + 2, 0, i + 1)
            window(NW - 1, 1, NPAIR, last=True)
            fed(NW - 1)
            v.wait_ge(s["yv"], NW + 1)
            v.wait_ge(s["base"], 2 * NW)
            step(nc.vector.tensor_scalar(wz[:, :], wz[:, :], 0.0, None, ALU.add))
            wz_i = wz[:, :].bitcast(I32)
            step(nc.vector.tensor_scalar(sel_m[:, :], wz_i, 31, 1, ALU.arith_shift_right, ALU.logical_shift_right))
            step(nc.vector.tensor_tensor(sel_i[:, :], wz_i, sel_m[:, :], ALU.bitwise_xor))
            step(nc.vector.tensor_scalar(sel_m[:, :], sel_i[:, :], -0x80000000, None, ALU.bitwise_xor))
            step(nc.vector.tensor_scalar(sel_i[:, :], sel_m[:, :], 16, None, ALU.logical_shift_right))
            step(nc.vector.tensor_copy(half_k[:, 0, :], sel_i[:, :]))
            step(nc.vector.tensor_scalar(sel_i[:, :], sel_m[:, :], 0xFFFF, None, ALU.bitwise_and))
            step(nc.vector.tensor_copy(half_k[:, 1, :], sel_i[:, :]))
            step(nc.vector.memset(thr[:, :], 0.0))
            counts = 0
            for part in range(2):
                if part:
                    step(nc.vector.tensor_scalar(mask[:, 0, :], half_k[:, 0, :], thr[:, 0:1], None, ALU.is_gt))
                    step(nc.vector.tensor_scalar(mask[:, 1, :], half_k[:, 0, :], thr[:, 0:1], None, ALU.is_equal))
                    step(nc.vector.scalar_tensor_tensor(half_k[:, 1, :], half_k[:, 1, :], 1.0, mask[:, 1, :], ALU.add, ALU.mult))
                    step(nc.vector.scalar_tensor_tensor(half_k[:, 1, :], mask[:, 0, :], 131072.0, half_k[:, 1, :], ALU.mult, ALU.add))
                    step(nc.vector.memset(thr[:, 1:2], 1.0))
                for bit in range(15, -1, -1):
                    step(nc.vector.tensor_scalar(tmp1[:, 0:1], thr[:, part:part + 1], float(1 << bit), None, ALU.add))
                    nc.vector.tensor_scalar(scr[:, :], half_k[:, part, :], tmp1[:, 0:1], None, ALU.is_ge, ALU.add,
                                            accum_out=csum[:, :]).then_inc(s["csum"], 1)
                    counts += 1
                    v.wait_ge(s["cntp"], 1 + counts)
                    step(nc.vector.tensor_scalar(tmp1[:, 1:2], bank[0][0:P, 0:1], float(KEEP), float(1 << bit), ALU.is_ge, ALU.mult))
                    step(nc.vector.tensor_tensor(thr[:, part:part + 1], thr[:, part:part + 1], tmp1[:, 1:2], ALU.add))
            step(nc.vector.tensor_scalar(mask[:, 1, :], half_k[:, 1, :], thr[:, 1:2], None, ALU.is_equal, ALU.add, accum_out=eqsum[:, :]))
            nc.vector.tensor_scalar(mask[:, 0, :], half_k[:, 1, :], thr[:, 1:2], None, ALU.is_gt, ALU.add,
                                    accum_out=csum[:, :]).then_inc(s["csum"], 1)
            step(nc.vector.tensor_tensor_scan(mask[:, 2, :], ones[0:P, 0:NW], mask[:, 1, :], 0.0, ALU.mult, ALU.add))
            v.wait_ge(s["cntp"], 34)
            step(nc.vector.tensor_scalar(tmp1[:, 0:1], bank[0][0:P, 0:1], -1.0, float(KEEP), ALU.mult, ALU.add))
            step(nc.vector.tensor_scalar(tmp1[:, 1:2], bank[1][0:P, 0:1], tmp1[:, 0:1], -1.0, ALU.subtract, ALU.mult))
            step(nc.vector.tensor_scalar(mask[:, 2, :], mask[:, 2, :], tmp1[:, 1:2], None, ALU.is_le))
            step(nc.vector.tensor_tensor(mask[:, 1, :], mask[:, 1, :], mask[:, 2, :], ALU.mult))
            step(nc.vector.tensor_tensor(mask[:, 0, :], mask[:, 0, :], mask[:, 1, :], ALU.add))
            step(nc.vector.tensor_tensor(coef[:, :], mask[:, 0, :], wz[:, :], ALU.mult))
            for w in range(NW):
                nc.vector.scalar_tensor_tensor(big_g[:, w, :], y_all[:, w, :], coef[:, w:w + 1], big_g[:, w, :],
                                               ALU.mult, ALU.add).then_inc(s["final"], 1)


_INS = ["x", "src", "dst", "L0_gnn_W", "L0_gnn_bias", "L0_mix_Wqkv", "L0_mix_Wproj", "L0_mix_bproj", "L0_mix_ln_g",
        "L0_mix_ln_b", "L0_mix_Wg1", "L0_mix_bg1", "L0_mix_Wg2", "L0_mix_bg2", "L0_ffn_wr", "L0_ffn_br",
        "L0_ffn_w1", "L0_ffn_b1", "L0_ffn_w2", "L0_ffn_b2"]


def kernel(**inputs):
    import numpy as _np
    import concourse.bacc as _bacc
    from concourse import mybir as _mybir
    from concourse.bass_utils import run_bass_kernel_spmd as _run

    nc = _bacc.Bacc("TRN2", target_bir_lowering=False, num_devices=1)
    arrays, args = {}, []
    for name in _INS:
        a = _np.ascontiguousarray(inputs[name])
        arrays[f"in_{name}"] = a
        args.append(nc.dram_tensor(f"in_{name}", a.shape, _mybir.dt.from_np(a.dtype), kind="ExternalInput").ap())
    args.append(nc.dram_tensor("out_0", (NODES, C), _mybir.dt.float32, kind="ExternalOutput").ap())
    gps_layer(nc, *args)
    r = _run(nc, [arrays], core_ids=[0])
    return r.results[0]["out_0"]
```

```python
import struct
from contextlib import ExitStack

import concourse.bass as bass
from concourse import mybir

F32 = mybir.dt.float32
BF16 = mybir.dt.bfloat16
I32 = mybir.dt.int32
ALU = mybir.AluOpType
ACT = mybir.ActivationFunctionType
AX = mybir.AxisListType

NODES, C, EDGES = 6250, 256, 100000
P = 125
NW = NODES // P
NPAIR = NW // 2
EP, EC = 125, EDGES // 125
GH = C // 4
HID = 4 * C
HC = HID // 128
KEEP = NODES // 2 - 1
EPS = 1e-5
TILE = 128
COLS = 1024
LOGF = 10
NB = 20
GROUP = 4
GEDGE = GROUP * TILE
ROUND = NB // GROUP
HOTS = 4
NOH = HOTS * GROUP
MAXG = COLS // GROUP
HCH = 200
NHIST = EC // HCH
COLBITS, ROWBITS = 13, 7
NOROW, NOWIN, BASE = 127, 63, 0x20000000
EMPTY = struct.unpack("<f", struct.pack("<I", BASE | NOWIN << COLBITS + ROWBITS | NOROW << COLBITS))[0]
PART = 3 * C
NEWTON = 3
SEARCH = 16
SORTED_BY = 19
PEEK4 = 7
LAST_PEEK = -(-PEEK4 * NW // 4)


def gps_layer(nc, x, src, dst, W, bias, Wqkv, Wproj, bproj, ln_g, ln_b, Wg1, bg1, Wg2, bg2,
              wr, br, w1, b1, w2, b2, out):
    table = nc.dram_tensor("table", (NODES, PART), BF16, kind="Internal").ap()
    ctx = ExitStack()
    with ctx:
        def sb(name, shape, dt=F32):
            return ctx.enter_context(nc.sbuf_tensor(name, shape, dt))

        def sem(name):
            return ctx.enter_context(nc.semaphore(name))

        bank = [ctx.enter_context(nc.psum_tensor(f"bank{i}", [128, 512], F32)) for i in range(8)]

        big_t = sb("big_t", [128, NW, C])
        big_g = sb("big_g", [P, NW, C])
        xnT = big_t[:, :, 0:2 * P].rearrange("p w (c n) -> p w c n", c=2)
        y_all = big_t[0:P, :, :]
        hot_row = big_t[0:EP, :, :].rearrange("p w c -> p (w c)").bitcast(BF16)[:, 0:P * HCH] \
            .rearrange("p (r j) -> p r j", j=HCH)
        keyA = sb("keyA", [128, COLS])
        keyB = sb("keyB", [128, COLS])
        col_of = sb("col_of", [128, COLS], I32)
        row_of = sb("row_of", [128, COLS])
        e_int = keyB[0:EP, 0:EC].bitcast(I32)
        gath = sb("gath", [128, NB, PART], BF16)
        qkv = gath[:, NB - 4:NB, :].rearrange("p s c -> p (s c)").bitcast(F32).rearrange("p (c n) -> p c n", c=2)
        gath_flat = gath[0:EP, :, :].rearrange("p s c -> p (s c)")
        hot_win = gath_flat[:, 0:NW * HCH].rearrange("p (w j) -> p w j", j=HCH)
        onehot = sb("onehot", [128, NOH, 128], BF16)
        onehot_g = onehot[:, :, :].rearrange("p (g u) r -> p g (u r)", u=GROUP)
        gath_g = gath[:, :, :].rearrange("p (g u) c -> p g (u c)", u=GROUP)
        idx_stage = sb("idx_stage", [128, NB], I32)
        sorted_keys = keyA
        row_b = onehot[0:EP, :, :].rearrange("p a b -> p (a b)")[:, 0:EC]
        win_b = onehot[0:EP, :, :].rearrange("p a b -> p (a b)")[:, 1024:1024 + EC]
        spent_all = onehot[:, :, :].rearrange("p a b -> p (a b)").bitcast(F32)
        iota_i = row_of[:, 0:128].bitcast(I32)
        iota_f = sb("iota_f", [128, 128])
        iota_b = sb("iota_b", [128, 128], BF16)
        part_i = sb("part_i", [128, 1], I32)
        part_f = sb("part_f", [128, 1])
        sign_i = sb("sign_i", [128, 8], I32)
        sign_t = sb("sign_t", [128, 8], I32)
        sign = sb("sign", [128, 8])
        ident = sb("ident", [128, 128])
        ident_b = sb("ident_b", [128, 128], BF16)
        lower = sb("lower", [128, 128])
        heads = sb("heads", [128, 128])
        ones = sb("ones", [128, 256])
        zeros_b = sb("zeros_b", [128, 264], BF16)
        zeros = zeros_b[:, :].bitcast(F32)
        W_in = sb("W_in", [128, 2, C])
        WT = sb("WT", [128, 2, C])
        WqT = sb("WqT", [128, 2, C])
        Wqc = sb("Wqc", [128, 2, C])
        proj = sb("proj", [128, 2, C])
        Wg1_in = sb("Wg1_in", [128, 2, GH])
        Wg1_g = sb("Wg1_g", [128, 2, GH])
        Wg2_b = sb("Wg2_b", [GH + 1, C])
        w1_sb = sb("w1_sb", [128, 2, HID])
        w2_sb = sb("w2_sb", [128, HC, C])
        lng = sb("lng", [128, 2])
        lnb = sb("lnb", [128, 2])
        lnb_wide = sb("lnb_wide", [128, 2, 128])
        b1_sb = sb("b1_sb", [128, HC])
        bg1_bc = sb("bg1_bc", [P, GH])
        bproj_bc = sb("bproj_bc", [P, C])
        b2_bc = sb("b2_bc", [P, C])
        wr_bc = sb("wr_bc", [P, C])
        br_bc = sb("br_bc", [P, 1])
        bn = sb("bn", [P, 2, 6])
        mv = sb("mv", [P, NW, 2])
        rstd = sb("rstd", [P, NW])
        nmr = sb("nmr", [P, NW])
        r2 = sb("r2", [P, NW])
        deg = sb("deg", [P, NW])
        norm = sb("norm", [P, NW])
        nwt = sb("nwt", [P, 3, NW])
        cnt = spent_all[:, 0 * NW:1 * NW]
        til = spent_all[:, 1 * NW:2 * NW]
        til_i = spent_all[:, 2 * NW:3 * NW].bitcast(I32)
        pad = spent_all[:, 3 * NW:4 * NW]
        pad_i = spent_all[:, 4 * NW:5 * NW].bitcast(I32)
        fill = spent_all[:, 6 * NW:7 * NW]
        scan = spent_all[:, 5 * NW:6 * NW]
        group_end = sb("group_end", [1, NW + 2], I32)
        xn = sb("xn", [P, 2, C])
        xT = sb("xT", [128, 2, 2, P])
        h_s = sb("h_s", [P, 2, C])
        h_res = sb("h_res", [P, 2, C])
        parts = sb("parts", [P, 2, 3, C], BF16)
        hg = sb("hg", [P, 2, GH])
        hgb = sb("hgb", [P, 2, GH])
        hact = sb("hact", [P, 2, GH])
        hgT = sb("hgT", [GH + 1, 2, P])
        kmax = sb("kmax", [128, 2])
        kmax2 = sb("kmax2", [128, 2])
        row_f = sb("row_f", [1, C])
        ones_b = sb("ones_b", [65, 128], BF16)
        rows_b = sb("rows_b", [65, C], BF16)
        ek = xn
        row_part = hg[0:1, :, :].rearrange("p a c -> p (a c)").bitcast(BF16)
        vv_all = sb("vv", [128, 2, 2, 129])
        vv = vv_all[0:P, :, :, :]
        rden = sb("rden", [128, 2])
        ctxn = lnb_wide
        xt = h_s
        hself = parts[:, :, :, :].rearrange("p j a c -> p j (a c)")
        og = h_res
        ogT = W_in[:, 1, 0:2 * P].rearrange("p (c n) -> p c n", c=2)
        xb = W_in[0:P, 0, :]
        xm = keyA[0:P, 0 * C:1 * C]
        wz1 = sb("wz1", [P, 1])
        x1 = keyA[0:P, 1 * C:2 * C]
        z = keyA[0:P, 2 * C:3 * C]
        zw = keyA[0:P, 3 * C:4 * C]
        zT = vv_all[:, :, :, :].rearrange("p a b n -> p (a b n)")[:, 0:2 * P].rearrange("p (c n) -> p c n", c=2)
        hid = keyB[:, 0:HC * P].rearrange("p (k n) -> p k n", k=HC)
        mv2 = sb("mv2", [P, 2])
        rs2 = sb("rs2", [P, 3])
        wz = sb("wz", [P, NW])
        spent = spent_all[0:P, :]
        sel_i = spent[:, 0:NW].bitcast(I32)
        sel_m = spent[:, NW:2 * NW].bitcast(I32)
        half_k = spent[:, 2 * NW:4 * NW].rearrange("p (a w) -> p a w", a=2)
        mask = spent[:, 4 * NW:7 * NW].rearrange("p (a w) -> p a w", a=3)
        scr = spent[:, 7 * NW:10 * NW].rearrange("p (a w) -> p a w", a=3)
        csum = sb("csum", [P, 3])
        eqsum = sb("eqsum", [P, 1])
        thr = sb("thr", [P, 2])
        want = sb("want", [P, 2])
        tmp1 = nwt[:, 0, 0:3]
        above = nwt[:, 1, 0:4]
        coef = spent[:, 10 * NW:11 * NW]

        names = ("edges wload xload const const2 wprep wtp wev hotr hist stats nwt bn bna bg1 kps cntp chain sortd keyp "
                 "tabs tabfree final issued outs xn tp xT main hgv hgb hact gtp ghT gps gate hev split hout xstore "
                 "kT kmaxd cntd kmt kmx kmr stage kv ekv ctxp ctxd ctxn wqcp wqcd idx oh arrived used selfused staged "
                 "op og otp ogT pp xb xm sum xh x1 st nt zed zwt ztp zT hp gelu yp yv base csum").split()
        s = {n: sem("s_" + n) for n in names}
        s_slot = [sem(f"s_slot{j}") for j in range(NB)]
        s_hself = [sem(f"s_hself{j}") for j in range(2)]
        s_xt = [sem(f"s_xt{j}") for j in range(2)]
        s_tab = [sem(f"s_tab{j}") for j in range(2)]
        block = ctx.enter_context(nc.Block())

        src_v = src.rearrange("(p j) -> p j", p=EP)
        dst_v = dst.rearrange("(p j) -> p j", p=EP)
        x_v = x.rearrange("(p w) c -> p w c", w=NW)
        out_v = out.rearrange("(p w) c -> p w c", w=NW)
        tab_v = table.rearrange("(p w) c -> p w c", w=NW)
        OUTW = 5

        @block.sync
        def _(sp):
            sp.dma_start(e_int, src_v).then_inc(s["edges"], 16)
            sp.dma_start(col_of[0:EP, 0:EC], dst_v).then_inc(s["edges"], 16)
            sp.dma_start(big_g[:, 0:25, :], x_v[:, 0:25, :]).then_inc(s["xload"], 16)
            sp.dma_start(big_g[:, 25:50, :], x_v[:, 25:50, :]).then_inc(s["xload"], 16)
            loads = [
                (W_in[:, :, :], W.rearrange("(o p) i -> p o i", p=128)),
                (qkv[:, :, :], Wqkv.rearrange("(c p) n -> p c n", p=128)),
                (proj[:, :, :], Wproj.rearrange("(c p) n -> p c n", p=128)),
                (Wg1_in[:, :, :], Wg1.rearrange("(c p) n -> p c n", p=128)),
                (Wg2_b[0:GH, :], Wg2),
                (Wg2_b[GH:GH + 1, :], bg2.rearrange("(a n) -> a n", a=1)),
                (w1_sb[:, :, :], w1.rearrange("(c p) n -> p c n", p=128)),
                (w2_sb[:, :, :], w2.rearrange("(c p) n -> p c n", p=128)),
                (row_f[:, :], bias.rearrange("(a n) -> a n", a=1)),
                (bg1_bc[:, :], bg1.rearrange("(a n) -> a n", a=1).to_broadcast([P, GH])),
                (bproj_bc[:, :], bproj.rearrange("(a n) -> a n", a=1).to_broadcast([P, C])),
                (b2_bc[:, :], b2.rearrange("(a n) -> a n", a=1).to_broadcast([P, C])),
                (wr_bc[:, :], wr.rearrange("n a -> a n").to_broadcast([P, C])),
                (br_bc[:, :], br.rearrange("(a n) -> a n", a=1).to_broadcast([P, 1])),
            ]
            for to, of in loads:
                sp.dma_start(to, of).then_inc(s["wload"], 16)
            with nc.allow_non_contiguous_dma(reason="three short vectors onto partitions"):
                sp.dma_start(lng[:, :], ln_g.rearrange("(c p) -> p c", p=128)).then_inc(s["wload"], 16)
                sp.dma_start(lnb[:, :], ln_b.rearrange("(c p) -> p c", p=128)).then_inc(s["wload"], 16)
                sp.dma_start(b1_sb[:, :], b1.rearrange("(c p) -> p c", p=128)).then_inc(s["wload"], 16)
            sp.sem_inc(s["tabfree"], 2)
            with sp.Fori(0, NPAIR) as i:
                for j in range(2):
                    sp.wait_ge(s["split"], i * 2 + (j + 3))
                    sp.dma_start(tab_v[:, bass.ds(i * 2 + j, 1), :].rearrange("p a c -> p (a c)"),
                                 parts[:, j, :, :].rearrange("p a c -> p (a c)")).then_inc(s_tab[j], 16)
                for j in range(2):
                    sp.wait_ge(s_tab[j], i * 16 + 16)
                    sp.sem_inc(s["tabfree"], 1)
            sp.wait_ge(s["tabs"], 2)
            sp.sem_inc(s["arrived"], ROUND)
            rounds = sp.value_load(group_end[0:1, NW + 1:NW + 2], min_val=1, max_val=COLS // NB)
            with sp.Fori(0, rounds) as i:
                for k in range(ROUND):
                    for j in range(k * GROUP, (k + 1) * GROUP):
                        sp.wait_ge(s_slot[j], i * 16 + 16)
                    sp.sem_inc(s["arrived"], 1)
            for g in range(NW // OUTW):
                sp.wait_ge(s["final"], (g + 1) * OUTW)
                sp.dma_start(out_v[:, g * OUTW:(g + 1) * OUTW, :],
                             big_g[:, g * OUTW:(g + 1) * OUTW, :]).then_inc(s["outs"], 16)
            sp.wait_ge(s["outs"], 16 * (NW // OUTW))

        @block.gpsimd
        def _(g):
            g.iota(iota_i[:, :], pattern=[[1, 128]], base=0, channel_multiplier=0).then_inc(s["const"], 1)
            g.iota(part_i[:, :], pattern=[[0, 1]], base=0, channel_multiplier=1).then_inc(s["const"], 1)
            g.memset(ident[:, :], 0.0).then_inc(s["const"], 1)
            g.memset(ones[:, :], 1.0).then_inc(s["const"], 1)
            g.memset(zeros[:, :], 0.0).then_inc(s["const"], 1)
            g.memset(vv_all[:, :, :, 128:129], 1.0).then_inc(s["const"], 1)
            g.wait_ge(s["const"], 6)
            g.affine_select(out=ident[:, :], in_=ident[:, :], compare_op=ALU.not_equal, fill=1.0, base=0,
                            pattern=[[-1, 128]], channel_multiplier=1).then_inc(s["const2"], 1)
            g.affine_select(out=lower[:, :], in_=ones[:, 0:128], compare_op=ALU.is_gt, fill=0.0, base=0,
                            pattern=[[1, 128]], channel_multiplier=-1).then_inc(s["const2"], 1)
            g.affine_select(out=heads[:, :], in_=ones[:, 0:128], compare_op=ALU.is_ge, fill=0.0, base=0,
                            pattern=[[-32, 4], [0, 32]], channel_multiplier=1).then_inc(s["const2"], 1)
            g.wait_ge(s["const2"], 3)
            g.affine_select(out=heads[:, :], in_=heads[:, :], compare_op=ALU.is_ge, fill=0.0, base=31,
                            pattern=[[32, 4], [0, 32]], channel_multiplier=-1).then_inc(s["const2"], 1)
            g.tensor_copy(ident_b[:, :], ident[:, :]).then_inc(s["const2"], 1)
            g.sem_inc(s["split"], 2)
            g.wait_ge(s["bg1"], 1)
            with g.Fori(0, NPAIR) as i:
                for j in range(2):
                    w = i * 2 + j
                    g.wait_ge(s["hgv"], w + 1)
                    g.sem_inc(s["issued"], 1)
                    g.tensor_tensor(hgb[:, j, :], hg[:, j, :], bg1_bc[:, :], ALU.add).then_inc(s["hgb"], 1)
                    g.wait_ge(s["hev"], w + 3)
                    g.sem_inc(s["issued"], 1)
                    g.tensor_tensor(h_res[:, j, :], h_s[:, j, :], parts[:, j, 0, :], ALU.subtract).then_inc(s["hout"], 1)
                    g.wait_ge(s["hout"], w * 2 + 1)
                    g.sem_inc(s["issued"], 1)
                    g.tensor_copy(parts[:, j, 1, :], h_res[:, j, :]).then_inc(s["hout"], 1)
                    g.wait_ge(s["hout"], w * 2 + 2)
                    g.sem_inc(s["issued"], 1)
                    g.tensor_tensor(parts[:, j, 2, :], h_res[:, j, :], parts[:, j, 1, :], ALU.subtract).then_inc(s["split"], 1)
            for j in range(2):
                g.wait_ge(s_tab[j], 16 * NPAIR)
            g.wait_ge(s["tabs"], 2)
            last_row = g.to_reg(NODES - 1)
            rounds = g.value_load(group_end[0:1, NW + 1:NW + 2], min_val=1, max_val=COLS // NB)
            with g.Fori(0, rounds) as i:
                for n, (lo, hi) in enumerate(((0, 2), (2, ROUND))):
                    g.wait_ge(s["arrived"], i * ROUND + hi)
                    g.sem_inc(s["issued"], 1)
                    g.tensor_copy(idx_stage[:, lo * GROUP:hi * GROUP],
                                  col_of[:, bass.ds(i * NB + lo * GROUP, (hi - lo) * GROUP)]).then_inc(s["idx"], 1)
                    g.wait_ge(s["idx"], i * 2 + (n + 1))
                    for k in range(lo, hi):
                        if k == ROUND - 1:
                            g.wait_ge(s["ctxd"], 1)
                        g.wait_ge(s["used"], i * ROUND + (k + 1))
                        g.sem_inc(s["issued"], 1)
                        for j in range(k * GROUP, (k + 1) * GROUP):
                            g.indirect_dma_start(
                                out=gath[:, j, :], out_offset=None, in_=table[:, :],
                                in_offset=bass.IndirectOffsetOnAxis(ap=idx_stage[:, j:j + 1], axis=0),
                                bounds_check=last_row, oob_is_err=True).then_inc(s_slot[j], 16)

        @block.scalar
        def _(a):
            for n, free in (("xstore", 2), ("hev", 2), ("ghT", 1), ("gate", 1), ("ekv", 4), ("ogT", 1), ("zT", 1), ("gelu", 1)):
                a.sem_inc(s[n], free)
            a.wait_ge(s["wload"], 16 * 17)
            for c in range(2):
                a.activation(Wg1_g[:, c, :], Wg1_in[:, c, :], ACT.Identity, scale=lng[:, c:c + 1]).then_inc(s["wev"], 1)
            a.wait_ge(s["wtp"], 1)
            a.activation(WT[:, :, :], bank[0][:, :].rearrange("p (c n) -> p c n", c=2), ACT.Copy).then_inc(s["wev"], 1)
            a.activation(WqT[:, :, :], bank[1][:, :].rearrange("p (c n) -> p c n", c=2), ACT.Copy).then_inc(s["wev"], 1)
            a.wait_ge(s["stats"], 1)
            def scaled(m, j):
                a.wait_ge(s["tp"], m + 1)
                a.sem_inc(s["issued"], 1)
                a.activation(xn[:, j, :], big_g[:, bass.ds(m, 1), :].rearrange("p a c -> p (a c)"), ACT.Identity,
                             bias=nmr[:, bass.ds(m, 1)], scale=rstd[:, bass.ds(m, 1)]).then_inc(s["xn"], 1)

            def turned(m, j):
                a.wait_ge(s["tp"], m + 3)
                a.wait_ge(s["kT"], m + 1)
                a.sem_inc(s["issued"], 1)
                xn_t = bank[j][:, 0:2 * P].rearrange("p (c n) -> p c n", c=2)
                a.activation(xT[:, j, :, :], xn_t, ACT.Copy).then_inc(s["xT"], 1)
                a.activation(xnT[:, bass.ds(m, 1), :, :].rearrange("p a c n -> p (a c) n"), xn_t,
                             ACT.Copy).then_inc(s["xstore"], 1)

            def produced(m, j):
                a.wait_ge(s["main"], m + 1)
                a.sem_inc(s["issued"], 1)
                a.activation(hg[:, j, :], bank[2 + j][0:P, 256:256 + GH], ACT.Identity,
                             scale=r2[:, bass.ds(m, 1)]).then_inc(s["hgv"], 1)

            def gate_turned(m, j):
                a.wait_ge(s["gtp"], m + 1)
                a.activation(hgT[0:GH, j, :], bank[5][0:GH, j * 128:j * 128 + P], ACT.Copy).then_inc(s["ghT"], 1)

            def h_out(m, j):
                a.wait_ge(s["split"], m + 1)
                a.wait_ge(s["tabfree"], m + 1)
                a.sem_inc(s["issued"], 1)
                a.activation(h_s[:, j, :], bank[2 + j][0:P, 0:C], ACT.Identity, scale=norm[:, bass.ds(m, 1)])
                a.activation(parts[:, j, 0, :], bank[2 + j][0:P, 0:C], ACT.Identity,
                             scale=norm[:, bass.ds(m, 1)]).then_inc(s["hev"], 1)

            def activated(m, j):
                a.wait_ge(s["hgb"], m + 1)
                a.activation(hact[:, j, :], hgb[:, j, :], ACT.Gelu).then_inc(s["hact"], 1)

            def gate_out(m):
                a.wait_ge(s["gps"], m + 1)
                a.sem_inc(s["issued"], 1)
                a.activation(big_g[:, bass.ds(m, 1), :].rearrange("p a c -> p (a c)"),
                             bank[6][0:P, 0:C], ACT.Tanh, scale=0.5).then_inc(s["gate"], 1)

            def pass_one(w, j, first=False, last=False, ahead=True):
                if not last:
                    turned(w + 1, 1 - j)
                produced(w, j)
                if not first:
                    gate_turned(w - 1, 1 - j)
                if ahead and not last:
                    scaled(w + 2, j)
                h_out(w, j)
                activated(w, j)
                if not first:
                    gate_out(w - 1)

            scaled(0, 0)
            scaled(1, 1)
            turned(0, 0)
            pass_one(0, 0, first=True)
            with a.Fori(0, NPAIR - 2) as i:
                pass_one(i * 2 + 1, 1)
                pass_one(i * 2 + 2, 0)
            pass_one(NW - 3, 1)
            pass_one(NW - 2, 0, ahead=False)
            pass_one(NW - 1, 1, last=True)
            gate_turned(NW - 1, 1)
            gate_out(NW - 1)
            a.wait_ge(s["kmt"], 1)
            a.activation(row_f[:, :], bank[5][0:1, 0:C], ACT.Copy, scale=-1.0).then_inc(s["kmx"], 1)
            def restage(m, j):
                a.wait_ge(s["kv"], m + 1)
                a.sem_inc(s["issued"], 1)
                a.activation(xT[:, j, :, :], xnT[:, bass.ds(m, 1), :, :].rearrange("p a c n -> p (a c) n"),
                             ACT.Copy).then_inc(s["stage"], 1)

            def exponents(m, j):
                a.wait_ge(s["kv"], m + 3)
                a.wait_ge(s["ctxp"], m + 1)
                a.activation(ek[:, j, :], bank[2 + j][0:P, 0:C], ACT.Exp).then_inc(s["ekv"], 1)
                a.activation(vv[:, j, :, 0:128], bank[2 + j][0:P, C:2 * C].rearrange("p (h n) -> p h n", h=2),
                             ACT.Copy).then_inc(s["ekv"], 1)

            a.activation(hact[:, 0, 0:1], hgb[:, 0, 0:1], ACT.Exp)
            restage(0, 0)
            restage(1, 1)
            with a.Fori(0, NPAIR - 1) as i:
                for j in range(2):
                    exponents(i * 2 + j, j)
                    restage(i * 2 + j + 2, j)
            exponents(NW - 2, 0)
            exponents(NW - 1, 1)
            for j in range(2):
                a.wait_ge(s_tab[j], 16 * NPAIR)

            def loads(m, j):
                a.wait_ge(s["selfused"], m + 1)
                a.dma_start(hself[:, j, :], tab_v[:, bass.ds(m, 1), :].rearrange("p a c -> p (a c)")).then_inc(s_hself[j], 16)
                a.wait_ge(s["xm"], m + 1)
                a.dma_start(xt[:, j, :], x_v[:, bass.ds(m, 1), :].rearrange("p a c -> p (a c)")).then_inc(s_xt[j], 16)

            def stage(m):
                a.wait_ge(s["op"], m + 1)
                a.sem_inc(s["issued"], 1)
                a.activation(xT[:, 0, :, :], xnT[:, bass.ds(m, 1), :, :].rearrange("p a c n -> p (a c) n"),
                             ACT.Copy).then_inc(s["staged"], 1)

            def gated(m):
                a.wait_ge(s["otp"], m + 2)
                a.activation(ogT[:, :, :], bank[2][:, 0:2 * P].rearrange("p (c n) -> p c n", c=2),
                             ACT.Copy).then_inc(s["ogT"], 1)

            def hidden(m):
                a.wait_ge(s["ztp"], m + 2)
                a.activation(zT[:, :, :], bank[4][:, 0:2 * P].rearrange("p (c n) -> p c n", c=2),
                             ACT.Copy).then_inc(s["zT"], 1)
                for k in range(HC):
                    if k % 4 == 0:
                        a.wait_ge(s["hp"], m * 2 + (k // 4 + 1))
                        a.wait_ge(s["yp"], m + 1)
                    a.activation(hid[:, k, :], bank[5 + k // 4][:, (k % 4) * P:(k % 4 + 1) * P], ACT.Gelu_apprx_tanh,
                                 bias=b1_sb[:, k:k + 1]).then_inc(s["gelu"], 1)

            def window(w, j, first=False, last=False):
                if not last:
                    loads(w + 1, 1 - j)
                    stage(w + 1)
                if not first:
                    hidden(w - 1)
                if not last:
                    gated(w + 1)

            loads(0, 0)
            a.wait_ge(s["wqcd"], 1)
            stage(0)
            a.activation(hact[:, 0, 0:1], hgb[:, 0, 0:1], ACT.Gelu_apprx_tanh)
            gated(0)
            window(0, 0, first=True)
            with a.Fori(0, NPAIR - 1) as i:
                window(i * 2 + 1, 1)
                window(i * 2 + 2, 0)
            window(NW - 1, 1, last=True)
            hidden(NW - 1)

        @block.tensor
        def _(t):
            for n, free in (("tp", 2), ("kT", 2), ("kv", 2), ("ctxp", 2), ("selfused", 2), ("used", ROUND), ("op", 1),
                            ("otp", 1), ("ztp", 1), ("yp", 1)):
                t.sem_inc(s[n], free)
            t.wait_ge(s["wload"], 16 * 17)
            t.wait_ge(s["const2"], 5)
            for c in range(2):
                for o in range(2):
                    t.transpose(bank[0][:, c * C + o * 128:c * C + (o + 1) * 128],
                                W_in[:, o, c * 128:(c + 1) * 128], ident[:, :])
            for c in range(2):
                for o in range(2):
                    last = t.transpose(bank[1][:, c * C + o * 128:c * C + (o + 1) * 128],
                                       qkv[:, o, c * 128:(c + 1) * 128], ident[:, :])
            last.then_inc(s["wtp"], 1)
            t.matmul(bank[3][0:P, 0:NW], ident_b[:, 0:P], zeros_b[:, 0:NW], start=True, stop=False, skip_group_check=True)
            with t.Fori(0, NHIST) as n:
                t.wait_ge(s["hotr"], n + 1)
                for u in range(HCH):
                    last = t.matmul(bank[3][0:P, 0:NW], hot_row[:, :, u], hot_win[:, :, u],
                                    start=False, stop=False, skip_group_check=True)
                last.then_inc(s["hist"], 1)
            t.matmul(bank[3][0:P, 0:NW], ident_b[:, 0:P], zeros_b[:, 0:NW], start=False, stop=True,
                     skip_group_check=True).then_inc(s["hist"], 1)
            t.wait_ge(s["wprep"], 1)
            for c in range(2):
                last = t.matmul(bank[2][0:P, 0:GH], lnb_wide[:, c, 0:P], Wg1_in[:, c, :], start=c == 0, stop=c == 1)
            last.then_inc(s["kps"], 1)
            t.wait_ge(s["nwt"], 1)
            t.matmul(bank[4][:, 0:NW], ones[0:P, 0:128], deg[:, :], start=True, stop=True).then_inc(s["cntp"], 1)
            t.wait_ge(s["wev"], 4)
            t.wait_ge(s["bg1"], 1)
            def turn(m, j):
                t.wait_ge(s["xn"], m + 1)
                t.wait_ge(s["xstore"], m + 1)
                for c in range(2):
                    last = t.transpose(bank[j][:, c * P:(c + 1) * P], xn[:, j, c * 128:(c + 1) * 128], ident[0:P, 0:P])
                last.then_inc(s["tp"], 1)

            def main(m, j):
                t.wait_ge(s["xT"], m + 1)
                t.wait_ge(s["hev"], m + 1)
                for c in range(2):
                    t.matmul(bank[2 + j][0:P, C:C + GH], xT[:, j, c, :], Wg1_g[:, c, :], start=c == 0, stop=c == 1)
                for c in range(2):
                    t.matmul(bank[2 + j][0:P, 0:C], xT[:, j, c, :], WT[:, c, :], start=c == 0, stop=False)
                t.matmul(bank[2 + j][0:P, 0:C], ones_b[:, 0:P], rows_b[:, :], start=False, stop=True).then_inc(s["main"], 1)

            def keys(m, j):
                t.wait_ge(s["kmaxd"], m + 1)
                for half in range(2):
                    for c in range(2):
                        last = t.matmul(bank[4 + 3 * j][:, half * P:(half + 1) * P],
                                        qkv[:, c, C + half * 128:C + (half + 1) * 128], xT[:, j, c, :],
                                        start=c == 0, stop=c == 1)
                last.then_inc(s["kT"], 1)

            def turn_gate(m, j):
                t.wait_ge(s["hact"], m + 1)
                t.wait_ge(s["ghT"], m + 1)
                t.sem_inc(s["issued"], 1)
                t.transpose(bank[5][0:GH, j * 128:j * 128 + P], hact[:, j, :], ident[0:P, 0:P]).then_inc(s["gtp"], 1)

            def gate(m, j):
                t.wait_ge(s["ghT"], m + 2)
                t.wait_ge(s["gate"], m + 1)
                t.matmul(bank[6][0:P, 0:C], hgT[:, j, :], Wg2_b[:, :], start=True, stop=True).then_inc(s["gps"], 1)

            def pass_one(w, j, first=False, last=False):
                if not last:
                    turn(w + 1, 1 - j)
                main(w, j)
                if not first:
                    turn_gate(w - 1, 1 - j)
                keys(w, j)
                if not first:
                    gate(w - 1, 1 - j)

            turn(0, 0)
            pass_one(0, 0, first=True)
            with t.Fori(0, NPAIR - 1) as i:
                pass_one(i * 2 + 1, 1)
                pass_one(i * 2 + 2, 0)
            pass_one(NW - 1, 1, last=True)
            turn_gate(NW - 1, 1)
            gate(NW - 1, 1)
            t.wait_ge(s["kmaxd"], NW + 2)
            t.wait_ge(s["gate"], NW + 1)
            for half in range(2):
                last = t.transpose(bank[5][0:1, half * 128:(half + 1) * 128], kmax[:, half:half + 1], ident[:, :])
            last.then_inc(s["kmt"], 1)
            for half in range(2):
                t.matmul(bank[6 + half][:, 0:129], ident[:, :], zeros[:, 0:129], start=True, stop=False, skip_group_check=True)
            t.wait_ge(s["kmr"], 1)

            def keys_values(m, j):
                t.wait_ge(s["stage"], m + 1)
                t.wait_ge(s["ekv"], m * 2 + 2)
                for c in range(2):
                    t.matmul(bank[2 + j][0:P, 0:C], xT[:, j, c, :], qkv[:, c, C:2 * C], start=c == 0, stop=False)
                t.matmul(bank[2 + j][0:P, 0:C], ones_b[:, 0:P], rows_b[:, :], start=False, stop=True)
                for c in range(2):
                    last = t.matmul(bank[2 + j][0:P, C:2 * C], xT[:, j, c, :], qkv[:, c, 2 * C:3 * C], start=c == 0, stop=c == 1)
                last.then_inc(s["kv"], 1)

            def contexts(m, j):
                t.wait_ge(s["ekv"], m * 2 + 6)
                for half in range(2):
                    last = t.matmul(bank[6 + half][:, 0:129], ek[:, j, half * 128:(half + 1) * 128], vv[:, j, half, :],
                                    start=False, stop=False, skip_group_check=True)
                last.then_inc(s["ctxp"], 1)

            keys_values(0, 0)
            def pair(i):
                keys_values(i * 2 + 1, 1)
                contexts(i * 2, 0)
                keys_values(i * 2 + 2, 0)
                contexts(i * 2 + 1, 1)

            with t.Fori(0, SORTED_BY) as i:
                pair(i)
            t.wait_ge(s["sortd"], 1)
            for b in range(COLS // 128):
                last = t.transpose(bank[b // 4][:, (b % 4) * 128:(b % 4 + 1) * 128], sorted_keys[:, b * 128:(b + 1) * 128], ident[:, :])
            last.then_inc(s["keyp"], 1)
            with t.Fori(SORTED_BY, NPAIR - 1) as i:
                pair(i)
            keys_values(NW - 1, 1)
            contexts(NW - 2, 0)
            contexts(NW - 1, 1)
            for half in range(2):
                last = t.matmul(bank[6 + half][:, 0:129], ident[:, :], zeros[:, 0:129], start=False, stop=True, skip_group_check=True)
            last.then_inc(s["ctxd"], 1)
            def sums(w, j, nth):
                first = t.value_load(group_end[0:1, bass.ds(w, 1)], min_val=0, max_val=MAXG - 1)
                end = t.value_load(group_end[0:1, bass.ds(w + 1, 1)], min_val=1, max_val=MAXG)
                t.wait_ge(s_hself[j], nth * 16 + 16)
                t.wait_ge(s["x1"], w + 1)
                t.matmul(bank[0][0:P, 0:2 * C], ident_b[0:P, 0:P], hself[:, j, 0:2 * C],
                         start=True, stop=False, skip_group_check=True)
                t.matmul(bank[0][0:P, 0:C], ident_b[0:P, 0:P], hself[:, j, 2 * C:3 * C],
                         start=False, stop=False, skip_group_check=True).then_inc(s["selfused"], 1)

                def group(q):
                    t.wait_ge(s["oh"], q + 1)
                    t.wait_ge(s["arrived"], q + (ROUND + 1))
                    slots, hot_slots = bass.ds(q % ROUND, 1), bass.ds(q % HOTS, 1)
                    for u in range(GROUP):
                        for lo, hi in ((2 * C, 3 * C), (0, 2 * C)):
                            last = t.matmul(bank[0][0:P, 0:hi - lo],
                                            onehot_g[:, hot_slots, u * 128:u * 128 + P].rearrange("p a r -> p (a r)"),
                                            gath_g[:, slots, u * PART + lo:u * PART + hi].rearrange("p a c -> p (a c)"),
                                            start=False, stop=False, skip_group_check=True)
                    last.then_inc(s["used"], 1)

                group(first)
                with t.Fori(first + 1, end) as q:
                    group(q)
                for half in range(2):
                    last = t.matmul(bank[0][0:P, half * C:(half + 1) * C], ident_b[:, 0:P], zeros_b[:, 0:C],
                                    start=False, stop=True, skip_group_check=True)
                last.then_inc(s["sum"], 1)

            def attention(m):
                t.wait_ge(s["staged"], m + 1)
                t.wait_ge(s["og"], m + 1)
                for c in range(2):
                    last = t.matmul(bank[1][0:P, 0:C], xT[:, 0, c, :], Wqc[:, c, :], start=c == 0, stop=c == 1)
                last.then_inc(s["op"], 1)

            def turn_gated(m):
                t.wait_ge(s["og"], m + 2)
                t.wait_ge(s["ogT"], m + 1)
                for c in range(2):
                    last = t.transpose(bank[2][:, c * P:(c + 1) * P], og[:, 0, c * 128:(c + 1) * 128], ident[0:P, 0:P])
                last.then_inc(s["otp"], 1)

            def project(m):
                t.wait_ge(s["ogT"], m + 2)
                t.wait_ge(s["xm"], m + 2)
                for c in range(2):
                    last = t.matmul(bank[3][0:P, 0:C], ogT[:, c, :], proj[:, c, :], start=c == 0, stop=c == 1)
                last.then_inc(s["pp"], 1)

            def turn_z(m):
                t.wait_ge(s["zed"], m + 1)
                t.wait_ge(s["zT"], m + 1)
                for c in range(2):
                    last = t.transpose(bank[4][:, c * P:(c + 1) * P], z[:, c * 128:(c + 1) * 128], ident[0:P, 0:P])
                last.then_inc(s["ztp"], 1)

            def up(m):
                t.wait_ge(s["zT"], m + 2)
                t.wait_ge(s["gelu"], m * HC + 1)
                for k in range(HC):
                    for c in range(2):
                        last = t.matmul(bank[5 + k // 4][:, (k % 4) * P:(k % 4 + 1) * P],
                                        w1_sb[:, c, k * 128:(k + 1) * 128], zT[:, c, :], start=c == 0, stop=c == 1)
                    if k % 4 == 3:
                        last.then_inc(s["hp"], 1)

            def down(m):
                t.wait_ge(s["yv"], m + 1)
                for k in range(HC):
                    if k % 4 == 0:
                        t.wait_ge(s["gelu"], m * HC + (k + 5))
                    last = t.matmul(bank[7][0:P, 0:C], hid[:, k, :], w2_sb[:, k, :], start=k == 0, stop=k == HC - 1)
                last.then_inc(s["yp"], 1)

            def window(w, j, nth, first=False, last=False):
                if not first:
                    sums(w, j, nth)
                    turn_z(w - 1)
                if not last:
                    attention(w + 1)
                if not first:
                    up(w - 1)
                if not last:
                    turn_gated(w + 1)
                if not first:
                    down(w - 1)
                if not last:
                    project(w + 1)

            t.wait_ge(s["tabs"], 2)
            sums(0, 0, 0)
            t.wait_ge(s["ctxn"], 1)
            for c in range(2):
                for half in range(2):
                    last = t.matmul(bank[4][:, c * C + half * 128:c * C + (half + 1) * 128],
                                    WqT[:, half, c * 128:(c + 1) * 128], ctxn[:, half, :], start=True, stop=True)
            last.then_inc(s["wqcp"], 1)
            t.wait_ge(s["wqcd"], 1)
            attention(0)
            turn_gated(0)
            project(0)
            window(0, 0, 0, first=True)
            with t.Fori(0, NPAIR - 1) as i:
                window(i * 2 + 1, 1, i)
                window(i * 2 + 2, 0, i + 1)
            window(NW - 1, 1, NPAIR - 1, last=True)
            for n in range(SEARCH):
                t.wait_ge(s["csum"], n + 1)
                t.matmul(bank[0][0:P, 0:3], ones[0:P, 0:P], csum[:, :], start=True, stop=True).then_inc(s["cntp"], 1)
            t.wait_ge(s["csum"], SEARCH + 1)
            t.matmul(bank[0][0:P, 0:1], ones[0:P, 0:P], csum[:, 0:1], start=True, stop=True)
            t.matmul(bank[1][0:P, 0:1], lower[0:P, 0:P], eqsum[:, :], start=True, stop=True).then_inc(s["cntp"], 1)
            turn_z(NW - 1)
            up(NW - 1)
            down(NW - 1)

        @block.vector
        def _(v):
            made = [0]

            def step(ins):
                made[0] += 1
                ins.then_inc(s["chain"], 1)
                v.wait_ge(s["chain"], made[0])

            v.wait_ge(s["const"], 6)
            step(nc.vector.memset(hgT[GH:GH + 1, :, :], 1.0))
            step(nc.vector.tensor_copy(iota_f[:, :], iota_i[:, :]))
            step(nc.vector.tensor_copy(iota_b[:, :], iota_f[:, :]))
            step(nc.vector.tensor_copy(part_f[:, :], part_i[:, :]))
            step(nc.vector.memset(ones_b[:, :], 1.0))
            step(nc.vector.memset(rows_b[:, :], 0.0))
            v.wait_ge(s["edges"], 32)
            step(nc.vector.tensor_copy(keyA[0:EP, 0:EC], e_int))
            row_i = row_of[0:EP, 0:EC].bitcast(I32)
            step(nc.vector.tensor_scalar(row_i, keyA[0:EP, 0:EC], 1.0 / NW, -0.49, ALU.mult, ALU.add))
            step(nc.vector.tensor_copy(row_b, row_i))
            step(nc.vector.scalar_tensor_tensor(keyA[0:EP, 0:EC], row_i, -float(NW), keyA[0:EP, 0:EC], ALU.mult, ALU.add))
            step(nc.vector.tensor_copy(win_b, keyA[0:EP, 0:EC]))
            step(nc.vector.tensor_copy(e_int, keyA[0:EP, 0:EC]))

            def histogram(n):
                if n:
                    v.wait_ge(s["hist"], n)
                at = slice(n * HCH, (n + 1) * HCH)
                for w in range(NW):
                    nc.vector.tensor_scalar(hot_win[:, w, :], win_b[:, at], float(w), None, ALU.is_equal)
                for r in range(P):
                    last = nc.vector.tensor_scalar(hot_row[:, r, :], row_b[:, at], float(r), None, ALU.is_equal)
                last.then_inc(s["hotr"], 1)

            def split_row(made_of, ready):
                v.wait_ge(s[made_of], ready)
                for k in range(3):
                    step(nc.vector.tensor_copy(rows_b[32 * k:32 * k + 1, :], row_f[:, :]))
                    if k < 2:
                        step(nc.vector.tensor_copy(row_part[:, :], row_f[:, :]))
                        step(nc.vector.tensor_tensor(row_f[:, :], row_f[:, :], row_part[:, :], ALU.subtract))

            def node_stats(w):
                nc.vector.bn_stats(bn[:, w % 2, :], big_g[:, w, :]).then_inc(s["bn"], 1)
                v.wait_ge(s["bn"], w + 1)
                nc.vector.bn_aggr(mv[:, w, :], bn[:, w % 2, :]).then_inc(s["bna"], 1)

            def inverse_sqrt(to, of, t):
                step(nc.vector.tensor_scalar(t.bitcast(I32), of.bitcast(I32), 1, None, ALU.logical_shift_right))
                step(nc.vector.tensor_scalar(to.bitcast(I32), t.bitcast(I32), -1.0, float(0x5F3759DF), ALU.mult, ALU.add))
                for _ in range(NEWTON):
                    step(nc.vector.tensor_tensor(t, to, to, ALU.mult))
                    step(nc.vector.tensor_tensor(t, t, of, ALU.mult))
                    step(nc.vector.tensor_scalar(t, t, -0.5, 1.5, ALU.mult, ALU.add))
                    step(nc.vector.tensor_tensor(to, to, t, ALU.mult))

            histogram(0)
            for m in range(8):
                step(nc.vector.tensor_scalar(sign_i[:, m:m + 1], part_i[:, :], max(m - 1, 0), None, ALU.logical_shift_right))
            for m in range(8):
                if m == 0:
                    step(nc.vector.tensor_copy(sign_t[:, m:m + 1], sign_i[:, m:m + 1]))
                else:
                    step(nc.vector.tensor_scalar(sign_t[:, m:m + 1], sign_i[:, m:m + 1], 1, None, ALU.logical_shift_right))
                    step(nc.vector.tensor_tensor(sign_t[:, m:m + 1], sign_t[:, m:m + 1], sign_i[:, m:m + 1], ALU.bitwise_xor))
            step(nc.vector.tensor_scalar(sign_t[:, :], sign_t[:, :], 1, None, ALU.bitwise_and))
            step(nc.vector.tensor_copy(sign[:, :], sign_t[:, :]))
            step(nc.vector.tensor_scalar(sign[:, :], sign[:, :], -2.0, 1.0, ALU.mult, ALU.add))
            step(nc.vector.memset(keyA[:, :], EMPTY))
            step(nc.vector.tensor_scalar(e_int, e_int, COLBITS + ROWBITS, BASE, ALU.logical_shift_left, ALU.bitwise_or))
            step(nc.vector.tensor_scalar(row_i, row_i, COLBITS, None, ALU.logical_shift_left))
            step(nc.vector.tensor_tensor(e_int, e_int, row_i, ALU.bitwise_or))
            step(nc.vector.tensor_tensor(keyA[0:EP, 0:EC].bitcast(I32), e_int, col_of[0:EP, 0:EC], ALU.bitwise_or))
            v.wait_ge(s["wload"], 16 * 17)
            for c in range(2):
                last = nc.vector.tensor_scalar(lnb_wide[:, c, :], ones[:, 0:128], lnb[:, c:c + 1], None, ALU.mult)
            last.then_inc(s["wprep"], 1)
            split_row("wload", 16 * 17)
            v.wait_ge(s["xload"], 32)
            for w in range(NW // 3):
                node_stats(w)
            histogram(1)
            for w in range(NW // 3, 2 * NW // 3):
                node_stats(w)
            histogram(2)
            for w in range(2 * NW // 3, NW):
                node_stats(w)
            v.wait_ge(s["bna"], NW)
            step(nc.vector.tensor_scalar(nwt[:, 0, :], mv[:, :, 1], EPS, None, ALU.add))
            inverse_sqrt(rstd[:, :], nwt[:, 0, :], nwt[:, 1, :])
            step(nc.vector.scalar_tensor_tensor(nmr[:, :], mv[:, :, 0], -1.0, rstd[:, :], ALU.mult, ALU.mult))
            step(nc.vector.tensor_tensor(nwt[:, 0, :], mv[:, :, 1], rstd[:, :], ALU.mult))
            step(nc.vector.tensor_tensor(nwt[:, 0, :], nwt[:, 0, :], rstd[:, :], ALU.mult))
            step(nc.vector.tensor_scalar(nwt[:, 0, :], nwt[:, 0, :], EPS, None, ALU.add))
            inverse_sqrt(r2[:, :], nwt[:, 0, :], nwt[:, 1, :])
            histogram(3)
            v.wait_ge(s["hist"], NHIST + 1)
            nc.vector.tensor_copy(deg[:, :], bank[3][0:P, 0:NW]).then_inc(s["nwt"], 1)
            v.wait_ge(s["nwt"], 1)
            step(nc.vector.tensor_scalar(nwt[:, 0, :], deg[:, :], 1.0, None, ALU.add))
            inverse_sqrt(norm[:, :], nwt[:, 0, :], nwt[:, 1, :])
            nc.vector.memset(kmax[:, :], -3.0e38).then_inc(s["stats"], 1)
            v.wait_ge(s["kps"], 1)
            nc.vector.tensor_tensor(bg1_bc[:, :], bank[2][0:P, 0:GH], bg1_bc[:, :], ALU.add).then_inc(s["bg1"], 1)
            v.wait_ge(s["cntp"], 1)
            nc.vector.tensor_copy(cnt[:, :], bank[4][:, 0:NW]).then_inc(s["cntd"], 1)
            v.wait_ge(s["cntd"], 1)
            v.sem_inc(s["kmaxd"], 2)
            step(nc.vector.tensor_scalar(til_i[:, :], cnt[:, :], 1.0 / GEDGE, 0.5 - 0.5 / GEDGE, ALU.mult, ALU.add))
            step(nc.vector.tensor_scalar(til[:, :], til_i[:, :], 1.0, None, ALU.max))
            step(nc.vector.scalar_tensor_tensor(pad[:, :], til[:, :], float(GEDGE), cnt[:, :], ALU.mult, ALU.subtract))
            step(nc.vector.tensor_scalar(cnt[:, :], iota_f[:, 0:NW], -float(NOWIN), None, ALU.add))
            for k in range(GROUP):
                step(nc.vector.tensor_scalar(fill[:, :], pad[:, :], -float(TILE * k), part_f[:, :], ALU.add, ALU.is_gt))
                step(nc.vector.tensor_tensor(fill[:, :], fill[:, :], cnt[:, :], ALU.mult))
                step(nc.vector.tensor_scalar(pad_i[:, :], fill[:, :], float(NOWIN), None, ALU.add))
                step(nc.vector.tensor_scalar(keyA[:, EC + k * NW:EC + (k + 1) * NW].bitcast(I32), pad_i[:, :],
                                             COLBITS + ROWBITS, BASE | NOROW << COLBITS,
                                             ALU.logical_shift_left, ALU.bitwise_or))
            step(nc.vector.tensor_tensor_scan(scan[:, :], ones[:, 0:NW], til[:, :], 0.0, ALU.mult, ALU.add))
            step(nc.vector.memset(group_end[:, 0:1], 0))
            step(nc.vector.tensor_copy(group_end[:, 1:NW], scan[0:1, 0:NW - 1]))
            step(nc.vector.tensor_scalar(group_end[:, NW + 1:NW + 2], scan[0:1, NW - 1:NW], 1.0 / ROUND,
                                         (ROUND - 1.0) / ROUND - 0.5 + 0.5 / ROUND, ALU.mult, ALU.add))
            step(nc.vector.tensor_scalar(group_end[:, NW:NW + 1], group_end[:, NW + 1:NW + 2], float(ROUND), None, ALU.mult))

            cur = [keyA, keyB]
            stages = [0]
            peeks = [0]

            def peek():
                n = peeks[0]
                if n < NW and stages[0] * 4 >= PEEK4 * (n + 1):
                    v.wait_ge(s["kT"], n + 3)
                    step(nc.vector.tensor_reduce(kmax2[:, :], bank[4 + 3 * (n % 2)][:, 0:2 * P].rearrange("p (h n) -> p h n", h=2),
                                                 AX.X, ALU.max))
                    nc.vector.tensor_tensor(kmax[:, :], kmax[:, :], kmax2[:, :], ALU.max).then_inc(s["kmaxd"], 1)
                    v.wait_ge(s["kmaxd"], n + 3)
                    peeks[0] += 1

            def exchange(lo_in, hi_in, lo_out, hi_out):
                nc.vector.tensor_tensor(lo_out, lo_in, hi_in, ALU.min).then_inc(s["chain"], 1)
                nc.vector.tensor_tensor(hi_out, lo_in, hi_in, ALU.max).then_inc(s["chain"], 1)
                made[0] += 2
                v.wait_ge(s["chain"], made[0])
                cur.reverse()
                stages[0] += 1
                peek()
                if stages[0] == LAST_PEEK + 6:
                    split_row("kmx", 1)
                    v.sem_inc(s["kmr"], 1)

            def distance(d):
                a, b = (k[:, :].rearrange("p (n two d) -> p n two d", two=2, d=d) for k in cur)
                exchange(a[:, :, 0, :], a[:, :, 1, :], b[:, :, 0, :], b[:, :, 1, :])

            def swap_blocks():
                step(nc.vector.transpose(cur[1][:, :], cur[0][:, :]))
                cur.reverse()

            def turn(m):
                step(nc.vector.tensor_scalar(cur[0][:, :], cur[0][:, :], sign[:, m:m + 1], None, ALU.mult))

            turn(0)
            for k in range(1, LOGF + 1):
                size = 1 << k
                a, b = (q[:, :].rearrange("p (n s) -> p n s", s=size) for q in cur)
                hi = a[:, :, size - 1:size // 2 - 1:-1] if size > 2 else a[:, :, 1:2]
                exchange(a[:, :, 0:size // 2], hi, b[:, :, 0:size // 2], b[:, :, size // 2:size])
                for e in range(k - 2, -1, -1):
                    distance(1 << e)
            for m in range(1, 8):
                turn(m)
                if m >= 7:
                    a, b = cur
                    step(nc.vector.tensor_tensor(b[0:64, :], a[0:64, :], a[64:128, :], ALU.min))
                    step(nc.vector.tensor_tensor(b[64:128, :], a[0:64, :], a[64:128, :], ALU.max))
                    cur.reverse()
                if m >= 6:
                    a, b = cur
                    for q in (0, 64):
                        step(nc.vector.tensor_tensor(b[q:q + 32, :], a[q:q + 32, :], a[q + 32:q + 64, :], ALU.min))
                        step(nc.vector.tensor_tensor(b[q + 32:q + 64, :], a[q:q + 32, :], a[q + 32:q + 64, :], ALU.max))
                    cur.reverse()
                swap_blocks()
                for e in range(min(m, 5) - 1, -1, -1):
                    distance(1 << e)
                swap_blocks()
                for e in range(LOGF - 1, 6 if m == 7 else -1, -1):
                    distance(1 << e)
            assert peeks[0] == NW and stages[0] > LAST_PEEK + 6
            assert cur[0] is sorted_keys
            v.sem_inc(s["sortd"], 1)
            v.wait_ge(s["keyp"], 1)
            spare = cur[1]
            for h in range(2):
                step(nc.vector.tensor_copy(spare[:, h * 512:(h + 1) * 512], bank[h][:, :]))
            keys_i = spare[:, :].bitcast(I32).rearrange("q (b p) -> q b p", b=8)
            nc.vector.tensor_scalar(col_of[:, :].rearrange("q (p b) -> q b p", b=8), keys_i, (1 << COLBITS) - 1, None,
                                    ALU.bitwise_and).then_inc(s["tabs"], 1)
            step(nc.vector.tensor_scalar(cur[0][:, :].bitcast(I32).rearrange("q (b p) -> q b p", b=8), keys_i, COLBITS,
                                         (1 << ROWBITS) - 1, ALU.logical_shift_right, ALU.bitwise_and))
            nc.vector.tensor_copy(row_of[:, :].rearrange("q (p b) -> q b p", b=8),
                                  cur[0][:, :].bitcast(I32).rearrange("q (b p) -> q b p", b=8)).then_inc(s["tabs"], 1)
            v.wait_ge(s["tabs"], 2)
            for n in ("x1", "og", "yv"):
                v.sem_inc(s[n], 1)
            v.sem_inc(s["xm"], 2)

            def hots(m):
                first = v.value_load(group_end[0:1, bass.ds(m, 1)], min_val=0, max_val=MAXG - 1)
                end = v.value_load(group_end[0:1, bass.ds(m + 1, 1)], min_val=1, max_val=MAXG)
                with v.Fori(first, end) as q:
                    v.wait_ge(s["used"], q + (ROUND - HOTS + 1))
                    slots = bass.ds(q % HOTS, 1)
                    for u in range(GROUP):
                        last = nc.vector.tensor_scalar(
                            onehot_g[:, slots, u * 128:u * 128 + P].rearrange("p a r -> p (a r)"),
                            iota_b[:, 0:P], row_of[:, bass.ds(q * GROUP + u, 1)], None, ALU.is_equal)
                    last.then_inc(s["oh"], 1)

            def gate_of(m):
                return big_g[:, bass.ds(m, 1), :].rearrange("p a c -> p (a c)")

            def gated(m):
                v.wait_ge(s["op"], m + 2)
                v.wait_ge(s["otp"], m + 1)
                nc.vector.scalar_tensor_tensor(og[:, 0, :], gate_of(m), 1.0, bank[1][0:P, 0:C],
                                               ALU.add, ALU.mult).then_inc(s["og"], 1)

            def mixed(m, j, nth):
                v.wait_ge(s_xt[j], nth * 16 + 16)
                nc.vector.tensor_tensor(xb[:, :], xt[:, j, :], bproj_bc[:, :], ALU.add).then_inc(s["xb"], 1)
                v.wait_ge(s["xb"], m + 1)
                v.wait_ge(s["pp"], m + 1)
                nc.vector.tensor_tensor(xm[:, :], bank[3][0:P, 0:C], xb[:, :], ALU.add).then_inc(s["xm"], 1)

            def normed(w):
                wi = bass.ds(w, 1)
                v.wait_ge(s["xm"], w + 3)
                v.wait_ge(s["sum"], w + 1)
                nc.vector.scalar_tensor_tensor(x1[:, :], bank[0][0:P, C:2 * C], norm[:, wi], xm[:, :],
                                               ALU.mult, ALU.add).then_inc(s["xh"], 1)
                v.wait_ge(s["xh"], w + 1)
                v.sem_inc(s["issued"], 1)
                nc.vector.scalar_tensor_tensor(x1[:, :], bank[0][0:P, 0:C], norm[:, wi], x1[:, :],
                                               ALU.mult, ALU.add).then_inc(s["x1"], 1)
                v.wait_ge(s["x1"], w + 2)
                nc.vector.bn_stats(bn[:, 0, :], x1[:, :]).then_inc(s["st"], 1)
                v.wait_ge(s["st"], w * 2 + 1)
                v.sem_inc(s["issued"], 1)
                nc.vector.bn_aggr(mv2[:, :], bn[:, 0, :]).then_inc(s["st"], 1)
                v.wait_ge(s["st"], w * 2 + 2)
                var, root, t0 = rs2[:, 0:1], rs2[:, 1:2], rs2[:, 2:3]
                ops = [lambda: nc.vector.tensor_scalar(var, mv2[:, 1:2], EPS, None, ALU.add),
                       lambda: nc.vector.tensor_scalar(t0.bitcast(I32), var.bitcast(I32), 1, None, ALU.logical_shift_right),
                       lambda: nc.vector.tensor_scalar(root.bitcast(I32), t0.bitcast(I32), -1.0, float(0x5F3759DF),
                                                       ALU.mult, ALU.add)]
                for _ in range(NEWTON):
                    ops += [lambda: nc.vector.tensor_scalar(t0, root, root, var, ALU.mult, ALU.mult),
                            lambda: nc.vector.tensor_scalar(t0, t0, -0.5, 1.5, ALU.mult, ALU.add),
                            lambda: nc.vector.tensor_tensor(root, root, t0, ALU.mult)]
                for n, op in enumerate(ops):
                    op().then_inc(s["nt"], 1)
                    v.wait_ge(s["nt"], w * len(ops) + (n + 1))
                v.wait_ge(s["ztp"], w + 1)
                nc.vector.tensor_scalar(z[:, :], x1[:, :], mv2[:, 0:1], root, ALU.subtract, ALU.mult).then_inc(s["zed"], 1)
                v.wait_ge(s["zed"], w + 1)
                nc.vector.tensor_tensor_reduce(out=zw[:, :], in0=z[:, :], in1=wr_bc[:, :], scale=1.0, scalar=0.0,
                                               op0=ALU.mult, op1=ALU.add, accum_out=wz1[:, :]).then_inc(s["zwt"], 1)
                nc.vector.tensor_tensor(gate_of(w), x1[:, :], z[:, :], ALU.add).then_inc(s["base"], 1)
                v.wait_ge(s["zwt"], w + 1)
                nc.vector.tensor_tensor(wz[:, wi], wz1[:, :], br_bc[:, :], ALU.add).then_inc(s["base"], 1)

            def fed(m):
                v.wait_ge(s["yp"], m + 2)
                nc.vector.tensor_tensor(y_all[:, bass.ds(m, 1), :].rearrange("p a c -> p (a c)"), bank[7][0:P, 0:C],
                                        b2_bc[:, :], ALU.add).then_inc(s["yv"], 1)

            def window(w, j, nth, first=False, last=False):
                if not last:
                    gated(w + 1)
                normed(w)
                if not last:
                    hots(w + 1)
                if not first:
                    fed(w - 1)
                if not last:
                    mixed(w + 1, 1 - j, nth)

            hots(0)
            v.wait_ge(s["ctxd"], 1)
            for half in range(2):
                step(nc.vector.reciprocal(rden[:, half:half + 1], bank[6 + half][:, 128:129]))
            for half in range(2):
                last = nc.vector.scalar_tensor_tensor(ctxn[:, half, :], bank[6 + half][:, 0:128], rden[:, half:half + 1],
                                                      heads[:, :], ALU.mult, ALU.mult)
                if half == 0:
                    step(last)
            last.then_inc(s["ctxn"], 1)
            v.wait_ge(s["wqcp"], 1)
            nc.vector.tensor_scalar(Wqc[:, :, :], bank[4][:, :].rearrange("p (c n) -> p c n", c=2), 0.5, None,
                                    ALU.mult).then_inc(s["wqcd"], 1)
            gated(0)
            mixed(0, 0, 0)
            window(0, 0, 0, first=True)
            with v.Fori(0, NPAIR - 1) as i:
                window(i * 2 + 1, 1, i + 1)
                window(i * 2 + 2, 0, i + 1)
            window(NW - 1, 1, NPAIR, last=True)
            v.wait_ge(s["yv"], NW)
            v.wait_ge(s["base"], 2 * NW)
            step(nc.vector.tensor_scalar(wz[:, :], wz[:, :], 0.0, None, ALU.add))
            wz_i = wz[:, :].bitcast(I32)
            step(nc.vector.tensor_scalar(sel_m[:, :], wz_i, 31, 1, ALU.arith_shift_right, ALU.logical_shift_right))
            step(nc.vector.tensor_tensor(sel_i[:, :], wz_i, sel_m[:, :], ALU.bitwise_xor))
            step(nc.vector.tensor_scalar(sel_m[:, :], sel_i[:, :], -0x80000000, None, ALU.bitwise_xor))
            step(nc.vector.tensor_scalar(sel_i[:, :], sel_m[:, :], 16, None, ALU.logical_shift_right))
            step(nc.vector.tensor_copy(half_k[:, 0, :], sel_i[:, :]))
            step(nc.vector.tensor_scalar(sel_i[:, :], sel_m[:, :], 0xFFFF, None, ALU.bitwise_and))
            step(nc.vector.tensor_copy(half_k[:, 1, :], sel_i[:, :]))
            step(nc.vector.memset(thr[:, :], 0.0))
            counts = 0
            for part in range(2):
                if part:
                    step(nc.vector.tensor_scalar(mask[:, 0, :], half_k[:, 0, :], thr[:, 0:1], None, ALU.is_gt))
                    step(nc.vector.tensor_scalar(mask[:, 1, :], half_k[:, 0, :], thr[:, 0:1], None, ALU.is_equal))
                    step(nc.vector.scalar_tensor_tensor(half_k[:, 1, :], half_k[:, 1, :], 1.0, mask[:, 1, :], ALU.add, ALU.mult))
                    step(nc.vector.scalar_tensor_tensor(half_k[:, 1, :], mask[:, 0, :], 131072.0, half_k[:, 1, :], ALU.mult, ALU.add))
                    step(nc.vector.memset(thr[:, 1:2], 1.0))
                for bit in range(14, -1, -2):
                    step(nc.vector.tensor_scalar(tmp1[:, :], iota_f[0:P, 1:4], float(1 << bit), thr[:, part:part + 1],
                                                 ALU.mult, ALU.add))
                    for k in range(3):
                        last = nc.vector.tensor_scalar(scr[:, k, :], half_k[:, part, :], tmp1[:, k:k + 1], None,
                                                       ALU.is_ge, ALU.add, accum_out=csum[:, k:k + 1])
                    last.then_inc(s["csum"], 1)
                    counts += 1
                    v.wait_ge(s["cntp"], 1 + counts)
                    step(nc.vector.tensor_scalar(above[:, 0:3], bank[0][0:P, 0:3], float(KEEP), None, ALU.is_ge, ALU.add,
                                                 accum_out=above[:, 3:4]))
                    step(nc.vector.scalar_tensor_tensor(thr[:, part:part + 1], above[:, 3:4], float(1 << bit),
                                                        thr[:, part:part + 1], ALU.mult, ALU.add))
            step(nc.vector.tensor_scalar(mask[:, 1, :], half_k[:, 1, :], thr[:, 1:2], None, ALU.is_equal, ALU.add, accum_out=eqsum[:, :]))
            nc.vector.tensor_scalar(mask[:, 0, :], half_k[:, 1, :], thr[:, 1:2], None, ALU.is_gt, ALU.add,
                                    accum_out=csum[:, 0:1]).then_inc(s["csum"], 1)
            step(nc.vector.tensor_tensor_scan(mask[:, 2, :], ones[0:P, 0:NW], mask[:, 1, :], 0.0, ALU.mult, ALU.add))
            v.wait_ge(s["cntp"], SEARCH + 2)
            step(nc.vector.tensor_scalar(tmp1[:, 0:1], bank[0][0:P, 0:1], -1.0, float(KEEP), ALU.mult, ALU.add))
            step(nc.vector.tensor_scalar(tmp1[:, 1:2], bank[1][0:P, 0:1], tmp1[:, 0:1], -1.0, ALU.subtract, ALU.mult))
            step(nc.vector.tensor_scalar(mask[:, 2, :], mask[:, 2, :], tmp1[:, 1:2], None, ALU.is_le))
            step(nc.vector.tensor_tensor(mask[:, 1, :], mask[:, 1, :], mask[:, 2, :], ALU.mult))
            step(nc.vector.tensor_tensor(mask[:, 0, :], mask[:, 0, :], mask[:, 1, :], ALU.add))
            step(nc.vector.tensor_tensor(coef[:, :], mask[:, 0, :], wz[:, :], ALU.mult))
            for w in range(NW):
                if w == NW - 1:
                    fed(w)
                    v.wait_ge(s["yv"], NW + 1)
                nc.vector.scalar_tensor_tensor(big_g[:, w, :], y_all[:, w, :], coef[:, w:w + 1], big_g[:, w, :],
                                               ALU.mult, ALU.add).then_inc(s["final"], 1)


_INS = ["x", "src", "dst", "L0_gnn_W", "L0_gnn_bias", "L0_mix_Wqkv", "L0_mix_Wproj", "L0_mix_bproj", "L0_mix_ln_g",
        "L0_mix_ln_b", "L0_mix_Wg1", "L0_mix_bg1", "L0_mix_Wg2", "L0_mix_bg2", "L0_ffn_wr", "L0_ffn_br",
        "L0_ffn_w1", "L0_ffn_b1", "L0_ffn_w2", "L0_ffn_b2"]


def kernel(**inputs):
    import numpy as _np
    import concourse.bacc as _bacc
    from concourse import mybir as _mybir
    from concourse.bass_utils import run_bass_kernel_spmd as _run

    nc = _bacc.Bacc("TRN2", target_bir_lowering=False, num_devices=1)
    arrays, args = {}, []
    for name in _INS:
        a = _np.ascontiguousarray(inputs[name])
        arrays[f"in_{name}"] = a
        args.append(nc.dram_tensor(f"in_{name}", a.shape, _mybir.dt.from_np(a.dtype), kind="ExternalInput").ap())
    args.append(nc.dram_tensor("out_0", (NODES, C), _mybir.dt.float32, kind="ExternalOutput").ap())
    gps_layer(nc, *args)
    r = _run(nc, [arrays], core_ids=[0])
    return r.results[0]["out_0"]
```
